# Optimizing a Trainium2 kernel written in Bass

```python
import numpy as np
import jax
import jax.numpy as jnp

def _softmax(x, axis=-1):
    return jax.nn.softmax(x, axis=axis)

def _gelu(x):
    return jax.nn.gelu(x, approximate=True)

def _silu(x):
    return jax.nn.silu(x)

def _sigmoid(x):
    return jax.nn.sigmoid(x)

def _layernorm(x, axis=-1, eps=1e-05):
    m = jnp.mean(x, axis=axis, keepdims=True)
    v = jnp.var(x, axis=axis, keepdims=True)
    return (x - m) / jnp.sqrt(v + eps)

def _scatter_add(tgt, idx, src, axis=0):
    return tgt.at[idx].add(src)

def _segment_sum(src, seg, n):
    return jax.ops.segment_sum(src, seg, n)
kernel_name = 'mk_gnn_resnorm_d2_gnn_r64_f6167a'

def setup_inputs(seed: int=0):
    np.random.seed(seed)
    _w = jnp.asarray

    def _rec_inputs():
        import jax
        import jax.numpy as jnp
        _gk = jax.random.key(seed)
        x = -0.000202 + 1 * jax.random.normal(jax.random.fold_in(_gk, 1), (50000, 128), jnp.float32)
        _s = jax.random.randint(jax.random.fold_in(_gk, 2), (6250,), 0, 50000, jnp.int32)
        _d = jax.random.randint(jax.random.fold_in(_gk, 3), (6250,), 0, 50000, jnp.int32)
        _loop = jnp.arange(50000, dtype=jnp.int32)
        src = jnp.concatenate([_s, _d, _loop])
        dst = jnp.concatenate([_d, _s, _loop])
        _o = jnp.argsort(dst, stable=True)
        src = src[_o]
        dst = dst[_o]
        return (x, src, dst)
    x, src, dst = _rec_inputs()

    def _L0_gnn_setup():
        import jax, jax.numpy as jnp
        import numpy as np
        N_NODES = 50000
        N_EDGES = 9375
        D = 128

        def _graphconv(h, src_idx, dst_idx, W, b, n_nodes):
            ones = jnp.ones_like(src_idx, dtype=h.dtype)
            deg_out = jax.ops.segment_sum(ones, src_idx, num_segments=n_nodes)
            deg_in = jax.ops.segment_sum(ones, dst_idx, num_segments=n_nodes)
            norm_src = jax.lax.rsqrt(jnp.maximum(deg_out, 1.0))
            norm_dst = jax.lax.rsqrt(jnp.maximum(deg_in, 1.0))
            hs = h * norm_src[:, None]
            msgs = hs[src_idx]
            agg = jax.ops.segment_sum(msgs, dst_idx, num_segments=n_nodes)
            return agg * norm_dst[:, None] @ W + b
        key = jax.random.key(seed)
        ks = jax.random.split(key, 6)
        x = jax.random.normal(ks[0], (N_NODES, D), dtype=jnp.float32)
        src_idx = jax.random.randint(ks[1], (N_EDGES,), 0, N_NODES, dtype=jnp.int64)
        dst_idx = jax.random.randint(ks[2], (N_EDGES,), 0, N_NODES, dtype=jnp.int64)
        W1 = jax.random.normal(ks[3], (D, D), dtype=jnp.float32) * (1.0 / np.sqrt(D))
        b1 = jnp.zeros((D,), dtype=jnp.float32)
        W2 = jax.random.normal(ks[4], (D, D), dtype=jnp.float32) * (1.0 / np.sqrt(D))
        b2 = jnp.zeros((D,), dtype=jnp.float32)
        return {'x': x, 'src_idx': src_idx, 'dst_idx': dst_idx, 'W1': W1, 'b1': b1, 'W2': W2, 'b2': b2}
    _L0_gnn_all = _L0_gnn_setup()
    _L0_gnn_in = {k: v for k, v in _L0_gnn_all.items() if k in ('W1', 'b1', 'W2', 'b2')}
    del _L0_gnn_all

    def _L1_gnn_setup():
        import jax, jax.numpy as jnp
        import numpy as np
        N_NODES = 50000
        N_EDGES = 12500
        D = 128

        def _mlp(h, W1, b1, W2, b2):
            return jax.nn.relu(h @ W1 + b1) @ W2 + b2
        key = jax.random.key(seed)
        ks = jax.random.split(key, 6)
        s = 0.05
        x = jax.random.normal(ks[0], (N_NODES, D), dtype=jnp.float32)
        edge_index = jax.random.randint(ks[1], (2, N_EDGES), 0, N_NODES, dtype=jnp.int64)
        We1 = jax.random.normal(ks[2], (2 * D, D), dtype=jnp.float32) * s
        be1 = jnp.zeros((D,), dtype=jnp.float32)
        We2 = jax.random.normal(ks[3], (D, D), dtype=jnp.float32) * s
        be2 = jnp.zeros((D,), dtype=jnp.float32)
        Wn1 = jax.random.normal(ks[4], (2 * D, D), dtype=jnp.float32) * s
        bn1 = jnp.zeros((D,), dtype=jnp.float32)
        Wn2 = jax.random.normal(ks[5], (D, D), dtype=jnp.float32) * s
        bn2 = jnp.zeros((D,), dtype=jnp.float32)
        return {'x': x, 'edge_index': edge_index, 'We1': We1, 'be1': be1, 'We2': We2, 'be2': be2, 'Wn1': Wn1, 'bn1': bn1, 'Wn2': Wn2, 'bn2': bn2}
    _L1_gnn_all = _L1_gnn_setup()
    _L1_gnn_in = {k: v for k, v in _L1_gnn_all.items() if k in ('We1', 'be1', 'We2', 'be2', 'Wn1', 'bn1', 'Wn2', 'bn2')}
    del _L1_gnn_all
    return {'x': x, 'src': src, 'dst': dst, 'L0_gnn_W1': _L0_gnn_in['W1'], 'L0_gnn_b1': _L0_gnn_in['b1'], 'L0_gnn_W2': _L0_gnn_in['W2'], 'L0_gnn_b2': _L0_gnn_in['b2'], 'L1_gnn_We1': _L1_gnn_in['We1'], 'L1_gnn_be1': _L1_gnn_in['be1'], 'L1_gnn_We2': _L1_gnn_in['We2'], 'L1_gnn_be2': _L1_gnn_in['be2'], 'L1_gnn_Wn1': _L1_gnn_in['Wn1'], 'L1_gnn_bn1': _L1_gnn_in['bn1'], 'L1_gnn_Wn2': _L1_gnn_in['Wn2'], 'L1_gnn_bn2': _L1_gnn_in['bn2']}

def reference(x, src, dst, L0_gnn_W1, L0_gnn_b1, L0_gnn_W2, L0_gnn_b2, L1_gnn_We1, L1_gnn_be1, L1_gnn_We2, L1_gnn_be2, L1_gnn_Wn1, L1_gnn_bn1, L1_gnn_Wn2, L1_gnn_bn2):
    import jax
    import jax.numpy as jnp

    def _L0_gnn_ref(x, src_idx, dst_idx, W1, b1, W2, b2):
        import jax, jax.numpy as jnp
        import numpy as np
        N_NODES = 50000
        N_EDGES = 9375
        D = 128

        def _graphconv(h, src_idx, dst_idx, W, b, n_nodes):
            ones = jnp.ones_like(src_idx, dtype=h.dtype)
            deg_out = jax.ops.segment_sum(ones, src_idx, num_segments=n_nodes)
            deg_in = jax.ops.segment_sum(ones, dst_idx, num_segments=n_nodes)
            norm_src = jax.lax.rsqrt(jnp.maximum(deg_out, 1.0))
            norm_dst = jax.lax.rsqrt(jnp.maximum(deg_in, 1.0))
            hs = h * norm_src[:, None]
            msgs = hs[src_idx]
            agg = jax.ops.segment_sum(msgs, dst_idx, num_segments=n_nodes)
            return agg * norm_dst[:, None] @ W + b
        n = x.shape[0]
        h = jax.nn.relu(_graphconv(x, src_idx, dst_idx, W1, b1, n))
        h = jax.nn.relu(_graphconv(h, src_idx, dst_idx, W2, b2, n))
        return h

    def _L1_gnn_ref(x, edge_index, We1, be1, We2, be2, Wn1, bn1, Wn2, bn2):
        import jax, jax.numpy as jnp
        import numpy as np
        N_NODES = 50000
        N_EDGES = 12500
        D = 128

        def _mlp(h, W1, b1, W2, b2):
            return jax.nn.relu(h @ W1 + b1) @ W2 + b2
        src = edge_index[0]
        dst = edge_index[1]
        e_in = jnp.concatenate([x[src], x[dst]], axis=-1)
        edge_new = _mlp(e_in, We1, be1, We2, be2)
        agg = jax.ops.segment_sum(edge_new, dst, num_segments=x.shape[0])
        mesh_new = _mlp(jnp.concatenate([x, agg], axis=-1), Wn1, bn1, Wn2, bn2)
        return x + mesh_new
    edge_index = jnp.stack([src, dst])
    x = _layernorm(x + _L0_gnn_ref(x, src, dst, L0_gnn_W1, L0_gnn_b1, L0_gnn_W2, L0_gnn_b2), axis=-1)
    x = _layernorm(x + _L1_gnn_ref(x, edge_index, L1_gnn_We1, L1_gnn_be1, L1_gnn_We2, L1_gnn_be2, L1_gnn_Wn1, L1_gnn_bn1, L1_gnn_Wn2, L1_gnn_bn2), axis=-1)
    return x

_drawn_inputs = setup_inputs


def setup_inputs(seed=0):
    import zlib

    import numpy as np

    out = dict(_drawn_inputs(seed))
    spreads = {'L0_gnn_b1': (0.0, 0.1),
     'L0_gnn_b2': (0.0, 0.1),
     'L1_gnn_be1': (0.0, 0.8),
     'L1_gnn_be2': (0.0, 0.54),
     'L1_gnn_bn1': (0.0, 0.433),
     'L1_gnn_bn2': (0.0, 0.1)}
    factors = {}
    for name, (base, spread) in spreads.items():
        noise = np.random.default_rng([zlib.crc32(name.encode()), seed]).standard_normal(out[name].shape)
        drawn = base * np.exp(spread * noise) if base else spread * noise
        out[name] = jnp.asarray(drawn.astype(out[name].dtype))
    for name, factor in factors.items():
        out[name] = (out[name] * factor).astype(out[name].dtype)
    return out
```

```python
from contextlib import ExitStack

import concourse.bass as bass
from concourse import mybir

F32 = mybir.dt.float32
BF16 = mybir.dt.bfloat16
I32 = mybir.dt.int32
I16 = mybir.dt.int16
ALU = mybir.AluOpType
ACT = mybir.ActivationFunctionType

P = 128
EPS = 1e-5


def gnn(nc, x, src, dst, W1, b1, W2, b2, We1, be1, We2, be2, Wn1, bn1, Wn2, bn2, out):
    N, D = x.shape
    E = src.shape[0]
    EP = 125
    ET = E // EP
    assert EP * ET == E and D == P
    B = 4
    GN = B * P
    G = -(-N // GN)
    NP = G * GN
    LASTP = (N - (G - 1) * GN) // B
    assert LASTP * B == N - (G - 1) * GN and G % 2 == 0
    TRASH = N

    with ExitStack() as ctx:
        def sb(name, shape, dt=F32):
            return ctx.enter_context(nc.sbuf_tensor(name, shape, dt))

        def ps(name, shape, dt=F32):
            return ctx.enter_context(nc.psum_tensor(name, shape, dt))

        def sem(name):
            return ctx.enter_context(nc.semaphore(name))

        def table(name, cols=D):
            return nc.dram_tensor(name, [NP, cols], F32, kind="Internal").ap()

        agg_tab = [table("agg1_tab"), table("agg2_tab"), table("relu_tab")]
        hs_tab = table("hs_tab")
        x1_tab = table("x1_tab")
        norm_tab = nc.dram_tensor("norm_tab", [P * G * B, 1], F32, kind="Internal").ap()
        deg_tab = nc.dram_tensor("deg_tab", [G * B, P], F32, kind="Internal").ap()

        src_i = sb("src_i", [EP, ET], I32)
        dst_i = sb("dst_i", [EP, ET], I32)
        nidx_i = sb("nidx_i", [EP, ET], I32)
        code = [sb(f"code{k}", [EP, ET]) for k in range(4)]
        tmp_i = [sb(f"tmp_i{k}", [EP, ET], I32) for k in range(2)]
        dst_f = sb("dst_f", [EP, ET])
        iota_c = sb("iota_c", [P, G * B], I16)
        iota_p = sb("iota_p", [P, 1])
        trash = sb("trash", [P, 1])
        ident = sb("ident", [P, P])
        lower = sb("lower", [P, P])
        ones = sb("ones", [P, P])
        hot = [sb(f"hot{k}", [P, 2, P], BF16) for k in range(2)]
        hotc = [sb(f"hotc{k}", [P, 2, G * B], BF16) for k in range(2)]
        deg_out = sb("deg_out", [P, G * B])
        deg_in = sb("deg_in", [P, G * B])
        nsrc = sb("nsrc", [P, G * B])
        ndst = sb("ndst", [P, G * B])
        rt = sb("rt", [P, G * B])
        degT = sb("degT", [P, 4, P])
        zero = sb("zero", [P, 3584])

        w1 = sb("w1", [P, D]); w2 = sb("w2", [P, D])
        we1a = sb("we1a", [P, D]); we1b = sb("we1b", [P, D]); we2 = sb("we2", [P, D])
        wn1a = sb("wn1a", [P, D]); wn1b = sb("wn1b", [P, D]); wn2 = sb("wn2", [P, D])
        we2T = sb("we2T", [P, D])
        wf = sb("wf", [P, D])
        be2c = sb("be2c", [P, 1]); bn1c = sb("bn1c", [P, 1])
        vrow = sb("vrow", [1, D])
        b1b = sb("b1b", [P, D]); b2b = sb("b2b", [P, D]); be1b = sb("be1b", [P, D]); bn2b = sb("bn2b", [P, D])

        col = sb("col", [EP, 4], I32)
        rows = sb("rows", [EP, 2, D])
        nrow = sb("nrow", [EP, 1])
        dstB = sb("dstB", [EP, EP])
        same = sb("same", [EP, EP])
        junk = sb("junk", [EP, EP])
        cnt = sb("cnt", [EP, 4])
        scat_i = sb("scat_i", [EP, 1], I32)
        msg = sb("msg", [EP, D])
        comb = sb("comb", [EP, D])
        edT = sb("edT", [P, 2, EP])

        ga = [sb(f"ga{k}", [P, B, D]) for k in range(2)]
        gx = [sb(f"gx{k}", [P, B, D]) for k in range(2)]
        gd = [sb(f"gd{k}", [1, GN]) for k in range(2)]
        aT = [sb(f"aT{k}", [P, GN]) for k in range(2)]
        xT = [sb(f"xT{k}", [P, GN]) for k in range(2)]
        mT = [sb(f"mT{k}", [P, GN]) for k in range(2)]
        y = [sb(f"y{k}", [P, B, D]) for k in range(2)]
        z = [sb(f"z{k}", [P, B, D]) for k in range(2)]
        go = [sb(f"go{k}", [P, B, D]) for k in range(2)]
        st = sb("st", [P, B, 6]); mv = sb("mv", [P, B, 2]); sd = sb("sd", [P, B]); rs = sb("rs", [P, B])
        eps = sb("eps", [P, 1])

        pA = [ps(f"pA{k}", [P, 512]) for k in range(2)]
        pB = [ps(f"pB{k}", [P, 512]) for k in range(2)]
        pC = [ps(f"pC{k}", [P, 512]) for k in range(2)]
        pD = [ps(f"pD{k}", [P, 512]) for k in range(2)]

        loaded = sem("loaded"); consts = sem("consts"); chain = sem("chain")
        held = sem("held"); held_dve = sem("held_dve"); zeroed = sem("zeroed"); zero_set = sem("zero_set")
        hot_ready = sem("hot_ready"); hist_done = sem("hist_done")
        deg_turn = sem("deg_turn"); deg_saved = sem("deg_saved"); norm_ready = sem("norm_ready"); tabs_saved = sem("tabs_saved")
        fuse_pe = sem("fuse_pe"); fuse_dve = sem("fuse_dve")
        col_ready = sem("col_ready"); rows_in = sem("rows_in"); rows2_in = sem("rows2_in"); nrow_in = sem("nrow_in")
        dst_spread = sem("dst_spread"); dst_turned = sem("dst_turned"); same_ready = sem("same_ready")
        scat_ready = sem("scat_ready"); msg_ready = sem("msg_ready"); summed = sem("summed"); comb_ready = sem("comb_ready")
        scattered = sem("scattered"); edge_turned = sem("edge_turned"); edge_copied = sem("edge_copied"); edge_mlp = sem("edge_mlp")
        edge_act = sem("edge_act")
        a_in = [[sem(f"a_in{s}{k}") for k in range(2)] for s in range(3)]
        x_in = [[sem(f"x_in{s}{k}") for k in range(2)] for s in range(3)]
        d_in = [sem(f"d_in{k}") for k in range(2)]
        turned = sem("turned"); copied = sem("copied"); mult = sem("mult"); hidden = sem("hidden"); mult2 = sem("mult2")
        group_out = [sem(f"group_out{k}") for k in range(2)]; var_ready = sem("var_ready"); sd_ready = sem("sd_ready"); y_ready = sem("y_ready")
        stored = [[sem(f"stored{s}{k}") for k in range(2)] for s in range(3)]
        loads_done = sem("loads_done")

        def groups(eng, body):
            with eng.Fori(0, G // 2 - 1) as i:
                body(2 * i, 0, i)
                body(2 * i + 1, 1, i)
            body(G - 2, 0, G // 2 - 1)
            body(G - 1, 1, G // 2 - 1)

        def rows_of(t, g):
            return t.rearrange("(g p i) d -> g p i d", p=P, i=B)[bass.ds(g, 1)].rearrange("g p i d -> (g p) i d")

        block = ctx.enter_context(nc.Block())

        LOADS = 2 + 8 + 2 + 4

        @block.sync
        def _(sp):
            sp.dma_start(src_i[:, :], src.rearrange("(p t) -> p t", p=EP)).then_inc(loaded, 16)
            sp.dma_start(dst_i[:, :], dst.rearrange("(p t) -> p t", p=EP)).then_inc(loaded, 16)
            for w, a in ((w1, W1), (w2, W2), (we1a, We1[0:P, :]), (we1b, We1[P:2 * P, :]), (we2, We2),
                         (wn1a, Wn1[0:P, :]), (wn1b, Wn1[P:2 * P, :]), (wn2, Wn2)):
                sp.dma_start(w[:, :], a).then_inc(loaded, 16)
            with nc.allow_non_contiguous_dma(reason="bias columns"):
                sp.dma_start(be2c[:, :], be2.rearrange("(p o) -> p o", o=1)).then_inc(loaded, 16)
                sp.dma_start(bn1c[:, :], bn1.rearrange("(p o) -> p o", o=1)).then_inc(loaded, 16)
            for w, a in ((b1b, b1), (b2b, b2), (be1b, be1), (bn2b, bn2)):
                sp.dma_start(w[:, :], a.rearrange("(o d) -> o d", o=1).to_broadcast([P, D])).then_inc(loaded, 16)
            sp.wait_ge(zero_set, 1)
            nz = 0
            for t in agg_tab:
                tz = t.rearrange("(c p q) d -> c p (q d)", p=P, q=3584 // D)
                for c in range(tz.shape[0]):
                    sp.dma_start(tz[c], zero[:, :]).then_inc(zeroed, 16)
                    nz += 1
            assert nz == 3 * NP * D // (P * 3584)
            sp.wait_ge(norm_ready, 2)
            sp.dma_start(norm_tab.rearrange("(p c) o -> p (c o)", p=P), nsrc[:, :]).then_inc(tabs_saved, 16)
            sp.wait_ge(deg_saved, 4)
            for c in range(4):
                m = min(P, G * B - c * P)
                sp.dma_start(deg_tab[c * P:c * P + m, :], degT[0:m, c, :]).then_inc(tabs_saved, 16)
            for s in range(3):
                sp.wait_ge(scattered, 16 * ET * (s + 1))
                if s == 2:
                    sp.wait_ge(tabs_saved, 16 * 5)

                def load(g, b, u, s=s):
                    sp.wait_ge(group_out[b], s * (G // 2) + u)
                    sp.dma_start(ga[b][:, :, :], rows_of(agg_tab[s], g)).then_inc(a_in[s][b], 16)
                    if s == 1:
                        if isinstance(g, int) and g == G - 1:
                            sp.dma_start(gx[b][0:LASTP, :, :], x[(G - 1) * GN:N, :].rearrange("(p i) d -> p i d", i=B)).then_inc(x_in[s][b], 16)
                        else:
                            sp.dma_start(gx[b][:, :, :], x[bass.ds(g * GN, GN), :].rearrange("(p i) d -> p i d", i=B)).then_inc(x_in[s][b], 16)
                    if s == 2:
                        sp.dma_start(gx[b][:, :, :], rows_of(x1_tab, g)).then_inc(x_in[s][b], 16)
                        sp.dma_start(gd[b][:, :], deg_tab.rearrange("(g i) p -> g (i p)", i=B)[bass.ds(g, 1), :]).then_inc(d_in[b], 16)
                groups(sp, load)

        @block.gpsimd
        def _(pool):
            nc.gpsimd.memset(zero[:, :], 0.0).then_inc(zero_set, 1)
            nc.gpsimd.memset(ones[:, :], 1.0).then_inc(consts, 1)
            nc.gpsimd.memset(eps[:, :], EPS).then_inc(consts, 1)
            nc.gpsimd.iota(iota_c[:, :], [[1, G * B]], base=0, channel_multiplier=0).then_inc(consts, 1)
            nc.gpsimd.iota(iota_p[:, :], [[0, 1]], base=0, channel_multiplier=1, allow_small_or_imprecise_dtypes=True).then_inc(consts, 1)
            nc.gpsimd.iota(trash[:, :], [[0, 1]], base=TRASH, channel_multiplier=1, allow_small_or_imprecise_dtypes=True).then_inc(consts, 1)
            pool.wait_ge(consts, 5)
            nc.gpsimd.affine_select(out=ident[:, :], in_=ones[:, :], compare_op=ALU.is_equal, fill=0.0,
                                    base=0, pattern=[[-1, P]], channel_multiplier=1).then_inc(consts, 1)
            nc.gpsimd.affine_select(out=lower[:, :], in_=ones[:, :], compare_op=ALU.is_gt, fill=0.0,
                                    base=0, pattern=[[-1, P]], channel_multiplier=1).then_inc(consts, 1)
            pool.wait_ge(zeroed, 16 * 42)
            pool.wait_ge(tabs_saved, 16 * 5)
            feat = [x, hs_tab, x1_tab]
            for s in range(3):
                if s:
                    for b in range(2):
                        pool.wait_ge(stored[s - 1][b], 16 * (G // 2))
                with pool.Fori(0, ET) as t:
                    nc.gpsimd.tensor_copy(col[:, 0:1], src_i[:, bass.ds(t, 1)])
                    nc.gpsimd.tensor_copy(col[:, 1:2], dst_i[:, bass.ds(t, 1)])
                    nc.gpsimd.tensor_copy(col[:, 2:3], nidx_i[:, bass.ds(t, 1)]).then_inc(col_ready, 1)
                    pool.wait_ge(col_ready, t + 1 + s * ET)
                    pool.sem_inc(held, 1)
                    nc.gpsimd.indirect_dma_start(out=rows[:, 0, :], out_offset=None, in_=feat[s][:, :],
                                                 in_offset=bass.IndirectOffsetOnAxis(ap=col[:, 0:1], axis=0)).then_inc(rows_in, 16)
                    if s == 0:
                        nc.gpsimd.indirect_dma_start(out=nrow[:, :], out_offset=None, in_=norm_tab[:, :],
                                                     in_offset=bass.IndirectOffsetOnAxis(ap=col[:, 2:3], axis=0)).then_inc(nrow_in, 16)
                    if s == 2:
                        nc.gpsimd.indirect_dma_start(out=rows[:, 1, :], out_offset=None, in_=feat[s][:, :],
                                                     in_offset=bass.IndirectOffsetOnAxis(ap=col[:, 1:2], axis=0)).then_inc(rows2_in, 16)
                    pool.wait_ge(scat_ready, t + 1 + s * ET)
                    pool.wait_ge(comb_ready, t + 1 + s * ET)
                    pool.sem_inc(held, 1)
                    nc.gpsimd.indirect_dma_start(out=agg_tab[s][:, :], out_offset=bass.IndirectOffsetOnAxis(ap=scat_i[:, 0:1], axis=0),
                                                 in_=comb[:, :], in_offset=None, compute_op=ALU.add).then_inc(scattered, 16)
                    pool.wait_ge(scattered, 16 * t + (16 + s * ET * 16))

        @block.vector
        def _(dve):
            n = [0]

            def step(ins):
                n[0] += 1
                ins.then_inc(chain, 1)
                dve.wait_ge(chain, n[0])

            dve.wait_ge(loaded, 16 * (LOADS))
            dve.wait_ge(consts, 7)
            for k, v in enumerate((src_i, dst_i)):
                step(nc.vector.tensor_scalar(tmp_i[0][:, :], v[:, :], 2, 127, ALU.logical_shift_right, ALU.bitwise_and))
                step(nc.vector.tensor_copy(code[2 * k][:, :], tmp_i[0][:, :]))
                step(nc.vector.tensor_scalar(tmp_i[0][:, :], v[:, :], 9, 2, ALU.logical_shift_right, ALU.logical_shift_left))
                step(nc.vector.tensor_scalar(tmp_i[1][:, :], v[:, :], 3, None, ALU.bitwise_and))
                step(nc.vector.tensor_tensor(code[2 * k + 1][:, :], tmp_i[0][:, :], tmp_i[1][:, :], ALU.add))
            step(nc.vector.scalar_tensor_tensor(nidx_i[:, :], code[0][:, :], float(G * B), code[1][:, :], ALU.mult, ALU.add))
            step(nc.vector.tensor_copy(dst_f[:, :], dst_i[:, :]))
            def hots(b, t, u):
                dve.wait_ge(hist_done, u)
                for k in range(2):
                    nc.vector.tensor_scalar(hot[b][0:EP, k, :], iota_c[0:EP, 0:P], code[2 * k][:, bass.ds(t, 1)], None, ALU.is_equal)
                    last = nc.vector.tensor_scalar(hotc[b][0:EP, k, :], iota_c[0:EP, :], code[2 * k + 1][:, bass.ds(t, 1)], None, ALU.is_equal)
                last.then_inc(hot_ready, 1)
            with dve.Fori(0, ET // 2) as i:
                hots(0, 2 * i, i)
                hots(1, 2 * i + 1, i)
            dve.wait_ge(hist_done, ET // 2)
            step(nc.vector.tensor_copy(deg_out[:, :], pA[0][:, 0:G * B]))
            step(nc.vector.tensor_copy(deg_in[:, :], pA[1][:, 0:G * B]))
            for k, (d, r) in enumerate(((deg_out, nsrc), (deg_in, ndst))):
                step(nc.vector.tensor_scalar(rt[:, :], d[:, :], 1.0, None, ALU.max))
                inv = nc.vector.reciprocal(r[:, :], rt[:, :])
                if k == 0:
                    step(inv)
            inv.then_inc(fuse_dve, 1)
            dve.wait_ge(deg_turn, 1)
            for c in range(4):
                m = min(P, G * B - c * P)
                nc.vector.tensor_copy(degT[0:m, c, :], pB[0][0:m, c * P:(c + 1) * P]).then_inc(deg_saved, 1)
            dve.wait_ge(fuse_pe, 1)
            nc.vector.tensor_copy(we2T[:, :], pB[1][:, 0:D]).then_inc(fuse_dve, 1)
            dve.wait_ge(fuse_pe, 2)
            nc.vector.tensor_copy(wf[:, :], pB[1][:, 128:128 + D])
            nc.vector.tensor_copy(vrow[:, :], pB[1][0:1, 256:256 + D]).then_inc(fuse_dve, 1)
            dve.wait_ge(norm_ready, 2)
            for s in range(3):
                with dve.Fori(0, ET) as t:
                    dve.wait_ge(comb_ready, t + s * ET)
                    dve.wait_ge(scattered, 16 * t + s * ET * 16)
                    nc.vector.tensor_copy(dstB[:, :], dst_f[:, bass.ds(t, 1)].to_broadcast([EP, EP]))
                    nc.vector.tensor_copy(cnt[:, 2:3], dst_f[:, bass.ds(t, 1)]).then_inc(dst_spread, 1)
                    dve.wait_ge(dst_turned, t + 1 + s * ET)
                    dve.wait_ge(dst_spread, t + 1 + s * ET)
                    nc.vector.tensor_scalar(same[:, :], pA[0][0:EP, 0:EP], cnt[:, 2:3], None, ALU.is_equal).then_inc(same_ready, 1)
                    dve.wait_ge(same_ready, t + 1 + s * ET)
                    nc.vector.tensor_tensor_reduce(out=junk[:, :], in0=same[:, :], in1=lower[0:EP, 0:EP], scale=1.0, scalar=0.0,
                                                   op0=ALU.mult, op1=ALU.add, accum_out=cnt[:, 0:1]).then_inc(chain, 1)
                    dve.wait_ge(chain, t * 4 + (n[0] + 1))
                    nc.vector.tensor_scalar(cnt[:, 1:2], cnt[:, 0:1], 0.5, None, ALU.is_lt).then_inc(chain, 1)
                    nc.vector.tensor_tensor(cnt[:, 3:4], cnt[:, 2:3], trash[0:EP, :], ALU.subtract).then_inc(chain, 1)
                    dve.wait_ge(chain, t * 4 + (n[0] + 3))
                    nc.vector.tensor_tensor(cnt[:, 0:1], cnt[:, 1:2], cnt[:, 3:4], ALU.mult).then_inc(chain, 1)
                    dve.wait_ge(chain, t * 4 + (n[0] + 4))
                    nc.vector.tensor_tensor(scat_i[:, :], cnt[:, 0:1], trash[0:EP, :], ALU.add).then_inc(scat_ready, 1)
                    if s == 0:
                        dve.wait_ge(rows_in, 16 * t + 16)
                        dve.wait_ge(nrow_in, 16 * t + 16)
                        nc.vector.tensor_scalar(msg[:, :], rows[:, 0, :], nrow[:, 0:1], None, ALU.mult).then_inc(msg_ready, 1)
                    if s == 2:
                        dve.wait_ge(edge_mlp, t + 1)
                        nc.vector.tensor_tensor(msg[:, :], pC[0][0:EP, 0:D], be1b[0:EP, :], ALU.add).then_inc(edge_act, 1)
                        dve.wait_ge(edge_act, t + 1)
                        nc.vector.tensor_scalar(msg[:, :], msg[:, :], 0.0, None, ALU.max).then_inc(msg_ready, 1)
                    dve.wait_ge(summed, t + 1 + s * ET)
                    nc.vector.tensor_copy(comb[:, :], pD[0][0:EP, 0:D]).then_inc(comb_ready, 1)
                n[0] += 4 * ET

                def bc(v, g):
                    return v[:, bass.ds(g * B, B)].rearrange("p (i o) -> p i o", o=1).to_broadcast([P, B, D])

                def bd(v):
                    return v[:, :].rearrange("p (o d) -> p o d", o=1).to_broadcast([P, B, D])

                per = {0: 3, 1: 5, 2: 4}[s]
                base = n[0]

                def post(g, b, u, s=s, per=per, base=base):
                    c = [0]

                    def link(ins):
                        c[0] += 1
                        ins.then_inc(chain, 1)
                        dve.wait_ge(chain, g * per + (base + c[0]))

                    def v3(t):
                        return t.rearrange("p (i d) -> p i d", i=B)

                    done = s * G + g
                    if s < 2:
                        dve.wait_ge(mult, done + 1)
                        link(nc.vector.tensor_tensor(y[b][:, :, :], v3(pB[b][:, :]), bc(ndst, g), ALU.mult))
                        link(nc.vector.tensor_tensor(z[b][:, :, :], y[b][:, :, :], bd(b1b if s == 0 else b2b), ALU.add))
                    if s == 0:
                        dve.wait_ge(stored[s][b], 16 * u)
                        link(nc.vector.tensor_scalar(y[b][:, :, :], z[b][:, :, :], 0.0, None, ALU.max))
                        last = nc.vector.tensor_tensor(go[b][:, :, :], y[b][:, :, :], bc(nsrc, g), ALU.mult)
                    else:
                        dve.wait_ge(x_in[s][b], 16 * u + 16)
                        if s == 1:
                            link(nc.vector.scalar_tensor_tensor(y[b][:, :, :], z[b][:, :, :], 0.0, gx[b][:, :, :], ALU.max, ALU.add))
                        else:
                            dve.wait_ge(mult2, g + 1)
                            link(nc.vector.tensor_tensor(z[b][:, :, :], v3(pD[b][:, :]), bd(bn2b), ALU.add))
                            link(nc.vector.scalar_tensor_tensor(y[b][:, :, :], gx[b][:, :, :], 2.0, z[b][:, :, :], ALU.mult, ALU.add))
                        for i in range(B):
                            last = nc.vector.bn_stats(st[:, i, :], y[b][:, i, :])
                        link(last)
                        dve.sem_inc(held_dve, 1)
                        for i in range(B):
                            last = nc.vector.bn_aggr(mv[:, i, :], st[:, i, :])
                        last.then_inc(var_ready, 1)
                        dve.wait_ge(sd_ready, (s - 1) * G + g + 1)
                        link(nc.vector.reciprocal(rs[:, :], sd[:, :]))
                        dve.wait_ge(stored[s][b], 16 * u)
                        for i in range(B):
                            last = nc.vector.tensor_scalar(go[b][:, i, :], y[b][:, i, :], mv[:, i, 0:1], rs[:, i:i + 1], ALU.subtract, ALU.mult)
                    assert c[0] == per
                    last.then_inc(group_out[b], 1)
                groups(dve, post)
                n[0] += per * G

        @block.scalar
        def _(act):
            act.wait_ge(fuse_dve, 1)
            nc.scalar.activation(nsrc[:, :], nsrc[:, :], ACT.Sqrt).then_inc(norm_ready, 1)
            nc.scalar.activation(ndst[:, :], ndst[:, :], ACT.Sqrt).then_inc(norm_ready, 1)
            for s in range(3):
                if s:
                    act.wait_ge(loaded, 16 * LOADS)
                if s == 2:
                    with act.Fori(0, ET) as t:
                        act.wait_ge(edge_turned, t + 1)
                        nc.scalar.copy(edT[:, :, :], pB[0][:, 0:2 * EP].rearrange("p (k e) -> p k e", k=2)).then_inc(edge_copied, 1)

                def pre(g, b, u, s=s):
                    act.wait_ge(turned, s * G + g + 1)
                    nc.scalar.copy(aT[b][:, :], pA[b][:, :]).then_inc(copied, 1)
                    if s == 2:
                        nc.scalar.copy(xT[b][:, :], pC[b][:, :]).then_inc(copied, 1)
                        act.wait_ge(mult, s * G + g + 1)
                        nc.scalar.activation(mT[b][:, :], pB[b][:, :], ACT.Relu, bias=bn1c[:, 0:1]).then_inc(hidden, 1)
                    if s:
                        act.wait_ge(var_ready, (s - 1) * G + g + 1)
                        nc.scalar.activation(sd[:, :], mv[:, :, 1], ACT.Sqrt, bias=eps[:, 0:1]).then_inc(sd_ready, 1)
                    act.wait_ge(group_out[b], s * (G // 2) + u + 1)
                    if s < 2:
                        act.dma_start(rows_of(hs_tab if s == 0 else x1_tab, g), go[b][:, :, :]).then_inc(stored[s][b], 16)
                    elif isinstance(g, int) and g == G - 1:
                        act.dma_start(out[(G - 1) * GN:N, :].rearrange("(p i) d -> p i d", i=B), go[b][0:LASTP, :, :]).then_inc(stored[s][b], 16)
                    else:
                        act.dma_start(out[bass.ds(g * GN, GN), :].rearrange("(p i) d -> p i d", i=B), go[b][:, :, :]).then_inc(stored[s][b], 16)
                groups(act, pre)
            for b in range(2):
                act.wait_ge(stored[2][b], 16 * (G // 2))

        @block.tensor
        def _(pe):
            def hist(b, t, i, start=False, stop=False):
                pe.wait_ge(hot_ready, t + 1)
                for k in range(2):
                    last = nc.tensor.matmul(pA[k][:, 0:G * B], hot[b][0:EP, k, :], hotc[b][0:EP, k, :], start=start, stop=stop)
                return last
            hist(0, 0, 0, start=True)
            hist(1, 1, 0).then_inc(hist_done, 1)
            with pe.Fori(1, ET // 2 - 1) as i:
                hist(0, 2 * i, i)
                hist(1, 2 * i + 1, i).then_inc(hist_done, 1)
            hist(0, ET - 2, 0)
            hist(1, ET - 1, 0, stop=True).then_inc(hist_done, 1)
            pe.wait_ge(fuse_dve, 1)
            for c in range(4):
                m = min(P, G * B - c * P)
                last = nc.tensor.transpose(pB[0][0:m, c * P:(c + 1) * P], deg_in[:, c * P:c * P + m], ident[:, :])
            last.then_inc(deg_turn, 1)
            nc.tensor.transpose(pB[1][:, 0:D], we2[:, :], ident[:, :]).then_inc(fuse_pe, 1)
            pe.wait_ge(fuse_dve, 2)
            nc.tensor.matmul(pB[1][:, 128:128 + D], we2T[:, :], wn1b[:, :], start=True, stop=True)
            nc.tensor.matmul(pB[1][0:1, 256:256 + D], be2c[:, :], wn1b[:, :], start=True, stop=True).then_inc(fuse_pe, 1)
            pe.wait_ge(fuse_dve, 3)
            pe.wait_ge(deg_saved, 4)
            for s in range(3):
                with pe.Fori(0, ET) as t:
                    pe.wait_ge(dst_spread, t + 1 + s * ET)
                    nc.tensor.transpose(pA[0][0:EP, 0:EP], dstB[:, :], ident[0:EP, 0:EP]).then_inc(dst_turned, 1)
                    if s == 2:
                        pe.wait_ge(rows_in, 16 * t + (16 + s * ET * 16))
                        pe.wait_ge(rows2_in, 16 * t + 16)
                        for k in range(2):
                            last = nc.tensor.transpose(pB[0][:, k * EP:(k + 1) * EP], rows[:, k, :], ident[0:EP, 0:EP])
                        last.then_inc(edge_turned, 1)
                        pe.wait_ge(edge_copied, t + 1)
                        nc.tensor.matmul(pC[0][0:EP, 0:D], edT[:, 0, :], we1a[:, :], start=True, stop=False)
                        nc.tensor.matmul(pC[0][0:EP, 0:D], edT[:, 1, :], we1b[:, :], start=False, stop=True).then_inc(edge_mlp, 1)
                    pe.wait_ge(same_ready, t + 1 + s * ET)
                    if s == 1:
                        pe.wait_ge(rows_in, 16 * t + (16 + s * ET * 16))
                        m = rows[:, 0, :]
                    else:
                        pe.wait_ge(msg_ready, t + 1 + (ET if s == 2 else 0))
                        m = msg[:, :]
                    nc.tensor.matmul(pD[0][0:EP, 0:D], same[:, :], m, start=True, stop=True).then_inc(summed, 1)

                def mm(g, b, u, s=s):
                    pe.wait_ge(group_out[b], s * (G // 2) + u)
                    pe.wait_ge(a_in[s][b], 16 * u + 16)
                    if s == 2:
                        pe.wait_ge(x_in[s][b], 16 * u + 16)
                    for i in range(B):
                        last = nc.tensor.transpose(pA[b][:, i * P:(i + 1) * P], ga[b][:, i, :], ident[:, :])
                        if s == 2:
                            last = nc.tensor.transpose(pC[b][:, i * P:(i + 1) * P], gx[b][:, i, :], ident[:, :])
                    last.then_inc(turned, 1)
                    if s < 2:
                        pe.wait_ge(copied, s * G + g + 1)
                        for i in range(B):
                            last = nc.tensor.matmul(pB[b][:, i * P:(i + 1) * P], aT[b][:, i * P:(i + 1) * P],
                                                    (w1 if s == 0 else w2)[:, :], start=True, stop=True)
                        last.then_inc(mult, 1)
                    else:
                        pe.wait_ge(copied, 2 * g + (2 * G + 2))
                        nc.tensor.matmul(pB[b][:, :], wn1a[:, :], xT[b][:, :], start=True, stop=False)
                        nc.tensor.matmul(pB[b][:, :], wf[:, :], aT[b][:, :], start=False, stop=False)
                        pe.wait_ge(d_in[b], 16 * u + 16)
                        nc.tensor.matmul(pB[b][:, :], vrow[:, :], gd[b][:, :], start=False, stop=True).then_inc(mult, 1)
                        pe.wait_ge(hidden, g + 1)
                        for i in range(B):
                            last = nc.tensor.matmul(pD[b][:, i * P:(i + 1) * P], mT[b][:, i * P:(i + 1) * P], wn2[:, :], start=True, stop=True)
                        last.then_inc(mult2, 1)
                groups(pe, mm)


_INS = ['x', 'src', 'dst', 'L0_gnn_W1', 'L0_gnn_b1', 'L0_gnn_W2', 'L0_gnn_b2', 'L1_gnn_We1', 'L1_gnn_be1', 'L1_gnn_We2',
        'L1_gnn_be2', 'L1_gnn_Wn1', 'L1_gnn_bn1', 'L1_gnn_Wn2', 'L1_gnn_bn2']


def kernel(**inputs):
    import numpy as _np
    import concourse.bacc as _bacc
    from concourse import mybir as _mybir
    from concourse.bass_utils import run_bass_kernel_spmd as _run

    nc = _bacc.Bacc("TRN2", target_bir_lowering=False, num_devices=1)
    arrays, args = {}, []
    for name in _INS:
        a = _np.ascontiguousarray(inputs[name])
        arrays[f"in_{name}_dram"] = a
        args.append(nc.dram_tensor(f"in_{name}_dram", a.shape, _mybir.dt.from_np(a.dtype), kind="ExternalInput").ap())
    args.append(nc.dram_tensor("out_0_dram", args[0].shape, F32, kind="ExternalOutput").ap())
    gnn(nc, *args)
    r = _run(nc, [arrays], core_ids=[0])
    return r.results[0]["out_0_dram"]
```

```python
from contextlib import ExitStack

import concourse.bass as bass
from concourse import mybir

F32 = mybir.dt.float32
BF16 = mybir.dt.bfloat16
I32 = mybir.dt.int32
F16 = mybir.dt.float16
ALU = mybir.AluOpType
ACT = mybir.ActivationFunctionType

P = 128
EPS = 1e-5


def gnn(nc, x, src, dst, W1, b1, W2, b2, We1, be1, We2, be2, Wn1, bn1, Wn2, bn2, out):
    N, D = x.shape
    E = src.shape[0]
    EP = 125
    ET = E // EP
    assert EP * ET == E and D == P
    B = 4
    GN = B * P
    G = -(-N // GN)
    NP = G * GN
    LASTP = (N - (G - 1) * GN) // B
    assert LASTP * B == N - (G - 1) * GN and G % 2 == 0
    TRASH = N

    with ExitStack() as ctx:
        def sb(name, shape, dt=F32):
            return ctx.enter_context(nc.sbuf_tensor(name, shape, dt))

        def ps(name, shape, dt=F32):
            return ctx.enter_context(nc.psum_tensor(name, shape, dt))

        def own(name):
            return ctx.enter_context(nc.semaphore(name))

        def table(name, cols=D):
            return nc.dram_tensor(name, [NP, cols], F32, kind="Internal").ap()

        agg_tab = [table("agg1_tab"), table("agg2_tab"), table("relu_tab")]
        hs_tab = table("hs_tab")
        x1_tab = table("x1_tab")
        norm_tab = nc.dram_tensor("norm_tab", [P * G * B, 1], F32, kind="Internal").ap()
        deg_tab = nc.dram_tensor("deg_tab", [G * B, P], F32, kind="Internal").ap()

        src_i = sb("src_i", [EP, ET], I32)
        dst_i = sb("dst_i", [EP, ET], I32)
        nidx_i = sb("nidx_i", [EP, ET], I32)
        code = [sb(f"code{k}", [EP, ET]) for k in range(4)]
        tmp_i = [sb(f"tmp_i{k}", [EP, ET], I32) for k in range(2)]
        dst_f = sb("dst_f", [EP, ET])
        iota_c = sb("iota_c", [P, G * B], F16)
        iota_p = sb("iota_p", [P, 1])
        trash = sb("trash", [P, 1])
        ident = sb("ident", [P, P])
        lower = sb("lower", [P, P])
        ones = sb("ones", [P, P])
        hot = [sb(f"hot{k}", [P, 2, P], BF16) for k in range(2)]
        hotc = [sb(f"hotc{k}", [P, 2, G * B], BF16) for k in range(2)]
        deg_out = sb("deg_out", [P, G * B])
        deg_in = sb("deg_in", [P, G * B])
        nsrc = sb("nsrc", [P, G * B])
        ndst = sb("ndst", [P, G * B])
        rt = sb("rt", [P, G * B])
        degT = sb("degT", [P, 4, P])
        zero = sb("zero", [P, 3584])

        w1 = sb("w1", [P, D]); w2 = sb("w2", [P, D])
        we1a = sb("we1a", [P, D]); we1b = sb("we1b", [P, D]); we2 = sb("we2", [P, D])
        wn1a = sb("wn1a", [P, D]); wn1b = sb("wn1b", [P, D]); wn2 = sb("wn2", [P, D])
        we2T = sb("we2T", [P, D])
        wf = sb("wf", [P, D])
        be2c = sb("be2c", [P, 1]); bn1c = sb("bn1c", [P, 1])
        vrow = sb("vrow", [1, D])
        b1b = sb("b1b", [P, D]); b2b = sb("b2b", [P, D]); be1b = sb("be1b", [P, D]); bn2b = sb("bn2b", [P, D])

        col = sb("col", [EP, 4], I32)
        rows = sb("rows", [EP, 2, D])
        nrow = sb("nrow", [EP, 1])
        dstB = sb("dstB", [EP, EP])
        same = sb("same", [EP, EP])
        junk = sb("junk", [EP, EP])
        cnt = sb("cnt", [EP, 4])
        scat_i = sb("scat_i", [EP, 1], I32)
        msg = sb("msg", [EP, D])
        comb = sb("comb", [EP, D])
        edT = sb("edT", [P, 2, EP])

        ga = [sb(f"ga{k}", [P, B, D]) for k in range(2)]
        gx = [sb(f"gx{k}", [P, B, D]) for k in range(2)]
        gd = [sb(f"gd{k}", [1, GN]) for k in range(2)]
        aT = [sb(f"aT{k}", [P, GN]) for k in range(2)]
        xT = [sb(f"xT{k}", [P, GN]) for k in range(2)]
        mT = [sb(f"mT{k}", [P, GN]) for k in range(2)]
        y = [sb(f"y{k}", [P, B, D]) for k in range(2)]
        z = [sb(f"z{k}", [P, B, D]) for k in range(2)]
        go = [sb(f"go{k}", [P, B, D]) for k in range(2)]
        st = sb("st", [P, B, 6]); mv = sb("mv", [P, B, 2]); sd = sb("sd", [P, B]); rs = sb("rs", [P, B])
        eps = sb("eps", [P, 1])

        pA = [ps(f"pA{k}", [P, 512]) for k in range(2)]
        pB = [ps(f"pB{k}", [P, 512]) for k in range(2)]
        pC = [ps(f"pC{k}", [P, 512]) for k in range(2)]
        pD = [ps(f"pD{k}", [P, 512]) for k in range(2)]

        loaded = own("loaded"); consts = own("consts"); chain = own("chain")
        held = own("held"); held_dve = own("held_dve")
        ctx_sem = ExitStack()

        def sem(name):
            return ctx_sem.enter_context(nc.semaphore(name))

        zeroed = sem("zeroed"); zero_set = sem("zero_set")
        hot_ready = sem("hot_ready"); hist_done = sem("hist_done")
        deg_turn = sem("deg_turn"); deg_saved = sem("deg_saved"); norm_ready = sem("norm_ready"); tabs_saved = sem("tabs_saved")
        fuse_pe = sem("fuse_pe"); fuse_dve = sem("fuse_dve")
        col_ready = sem("col_ready"); rows_in = sem("rows_in"); rows2_in = sem("rows2_in"); nrow_in = sem("nrow_in")
        dst_spread = sem("dst_spread"); dst_turned = sem("dst_turned"); same_ready = sem("same_ready")
        scat_ready = sem("scat_ready"); msg_ready = sem("msg_ready"); summed = sem("summed"); comb_ready = sem("comb_ready")
        scattered = sem("scattered"); edge_turned = sem("edge_turned"); edge_copied = sem("edge_copied"); edge_mlp = sem("edge_mlp")
        edge_act = sem("edge_act")
        a_in = [[sem(f"a_in{s}{k}") for k in range(2)] for s in range(3)]
        x_in = [[sem(f"x_in{s}{k}") for k in range(2)] for s in range(3)]
        d_in = [sem(f"d_in{k}") for k in range(2)]
        turned = sem("turned"); copied = sem("copied"); mult = sem("mult"); hidden = sem("hidden"); mult2 = sem("mult2")
        group_out = [sem(f"group_out{k}") for k in range(2)]; var_ready = sem("var_ready"); sd_ready = sem("sd_ready")
        stored = [[sem(f"stored{s}{k}") for k in range(2)] for s in range(3)]
        ctx_sem.close()

        def tiles(eng, body):
            body(0)
            with eng.Fori(1, ET) as t:
                body(t)

        def wait(eng, semaphore, value):
            if not (isinstance(value, int) and value <= 0):
                eng.wait_ge(semaphore, value)

        def groups(eng, body):
            body(0, 0, 0)
            body(1, 1, 0)
            with eng.Fori(1, G // 2 - 1) as i:
                body(2 * i, 0, i)
                body(2 * i + 1, 1, i)
            body(G - 2, 0, G // 2 - 1)
            body(G - 1, 1, G // 2 - 1)

        def rows_of(t, g):
            return t.rearrange("(g p i) d -> g p i d", p=P, i=B)[bass.ds(g, 1)].rearrange("g p i d -> (g p) i d")



        SLOTS = P
        HN = GN // 2
        T = 2 * G
        WIN = HN + SLOTS
        CS = 100
        CW = WIN + CS
        CL = (E - CW) // CS + 1
        KEY = 1 << 16

        win_tab = [nc.dram_tensor(f"win_tab{k}", [CL + 1, CW], I32, kind="Internal").ap() for k in range(2)]
        vpart_tab = nc.dram_tensor("vpart_tab", [6, D], BF16, kind="Internal").ap()
        deg16_tab = nc.dram_tensor("deg16_tab", [G * B, P], BF16, kind="Internal").ap()

        regular_i = sb("regular_i", [1, 4], I32)
        upper = sb("upper", [P, P])
        edge_f, loop, rank = code[0:2], code[2], code[3]
        off1 = sb("off1", [P, 1])
        check = sb("check", [P, 8])
        verdict = sb("verdict", [1, 8])
        tile_first = sb("tile_first", [P, 2, G])
        below = sb("below", [EP, 5, 2, G], BF16)
        onesb = sb("onesb", [P, P], BF16)
        first_win = sb("first_win", [P, 2])
        first_i = sb("first_i", [P, 2], I32)
        my_first = sb("my_first", [P, 2])
        win_i = [sb(f"win_i{k}", [P, 2, CW], I32) for k in range(2)]
        win_f = [sb(f"win_f{k}", [P, 2, CW]) for k in range(2)]
        wa = sb("wa", [P, 2, CW])
        wb = sb("wb", [P, 2, CW])
        keys = sb("keys", [P, 2, SLOTS])
        kT = sb("kT", [P, 2, G], I32)
        t0 = sb("t0", [P, 2, G], I32); t1 = sb("t1", [P, 2, G], I32); t2 = sb("t2", [P, 2, G], I32)
        sidx = sb("sidx", [P, 2, G], I32)
        didx = sb("didx", [P, 2, G], I32)
        nidx = sb("nidx", [P, 2, G], I32)
        dcode = sb("dcode", [P, 2, G])
        srow = sb("srow", [P, 2, G]); scol = sb("scol", [P, 2, G])
        dq = sb("dq", [P, 2, G], BF16)
        di = sb("di", [P, 2, G], BF16)
        iota_b = sb("iota_b", [P, HN], BF16)
        hp = zero[:, 0:G * 32].bitcast(BF16).rearrange("p (g q) -> p g q", g=G)
        hi = sb("hi", [P, G, B], BF16)
        degT16 = sb("degT16", [P, 4, P], BF16)
        wes = sb("wes", [P, D])
        be1c = sb("be1c", [P, 1])
        be1r = sb("be1r", [1, D])
        vparts = sb("vparts", [1, 6, D], BF16)
        vres = sb("vres", [1, 2, D])
        vp3 = sb("vp3", [3, 2, D], BF16)
        fcol = [sb(f"fcol{r}", [P, 4], I32) for r in range(4)]
        fx = [sb(f"fx{r}", [P, B, D]) for r in range(4)]
        fx2 = [sb(f"fx2{r}", [P, B, D]) for r in range(4)]
        fr = [sb(f"fr{r}", [P, 4, D]) for r in range(4)]
        fn = [sb(f"fn{r}", [P, 2]) for r in range(4)]
        fd = [sb(f"fd{r}", [3, GN], BF16) for r in range(4)]
        fhot = [sb(f"fhot{r}", [P, 2, HN]) for r in range(2)]
        fy = [sb(f"fy{r}", [P, B, D]) for r in range(4)]
        fe = [sb(f"fe{r}", [P, GN]) for r in range(2)]
        fs = [sb(f"fs{r}", [P, GN]) for r in range(2)]
        fm = [sb(f"fm{r}", [P, 2, D]) for r in range(2)]
        fst = [sb(f"fst{r}", [P, B, 6]) for r in range(4)]
        fmv = [sb(f"fmv{r}", [P, B, 2]) for r in range(4)]
        fsd = [sb(f"fsd{r}", [P, B]) for r in range(4)]
        frs = [sb(f"frs{r}", [P, B]) for r in range(4)]
        fnm = [sb(f"fnm{r}", [P, B]) for r in range(4)]

        ranked = own("ranked"); rank_off = own("rank_off"); win_built = own("win_built"); below_set = own("below_set")
        counted = own("counted"); first_set = own("first_set"); win_in = own("win_in"); checked = own("checked"); check_sum = own("check_sum")
        verdict_set = own("verdict_set")
        keys_set = own("keys_set"); keys_turned = own("keys_turned"); slots_set = own("slots_set")
        f_hot = own("f_hot"); f_hist = own("f_hist"); f_hp = own("f_hp"); f_in = own("f_in"); f_recip = own("f_recip"); f_norm = own("f_norm")
        f_degt = own("f_degt"); f_deg16 = own("f_deg16"); f_tabs = own("f_tabs"); f_fuse_pe = own("f_fuse_pe"); f_fuse = own("f_fuse"); f_parts = own("f_parts"); f_parts_in = own("f_parts_in")
        f_clean = own("f_clean")

        class Phase:
            def __init__(self, s):
                def four(name):
                    return [own(f"{name}_{s}_{r}") for r in range(4)]
                self.x_in = four("rows_of_group")
                self.x2_in = four("x_of_group") if s == 1 else None
                self.d_in = four("degrees_of_group") if s == 2 else None
                self.gathered = four("gathered")
                self.stored = [own(f"stored_{s}_{r}") for r in range(2)]
                self.col_set = own(f"col_set_{s}")
                self.hot_set = own(f"hot_set_{s}")
                self.summed = own(f"summed_{s}")
                self.evacuated = own(f"evacuated_{s}")
                self.mixed = own(f"mixed_{s}")
                self.scaled = own(f"scaled_{s}")
                self.rsum = own(f"rsum_{s}")
                self.radd = own(f"radd_{s}")
                self.hid = own(f"hid_{s}")
                self.hidact = own(f"hidact_{s}")
                self.outp = own(f"outp_{s}")
                self.posted = own(f"posted_{s}")
                self.rooted = own(f"rooted_{s}")
                self.recip = own(f"recip_{s}")
                self.inverted = own(f"inverted_{s}")
                self.result = own(f"result_{s}")
        phases = [Phase(s) for s in range(3)]

        LOADS = 2 + 8 + 2 + 4 + 2
        class At:

            def __init__(self, g, r, u):
                self.g, self.r, self.u = g, r, u
                self.b = r % 2
                self.half = 2 * u + r // 2

        def pipeline(eng, body, lead, lag):
            def fixed(j):
                def at(d):
                    g = j + d
                    return At(g, g % 4, g // 4) if 0 <= g < G else None
                return at

            def turning(i, jm):
                def at(d):
                    k = jm + d
                    return At(4 * i + k, k % 4, i + k // 4)
                return at
            for j in range(-lead, 4):
                body(fixed(j))
            with eng.Fori(1, G // 4) as i:
                for jm in range(4):
                    body(turning(i, jm))
            for j in range(4 * (G // 4), G + lag):
                body(fixed(j))

        def after(eng, semaphore, at, back=0):
            wait(eng, semaphore, at.g + (1 - back))

        def landed(eng, semaphore, at, dmas=1, back=0):
            wait(eng, semaphore[at.r], at.u * (16 * dmas) + 16 * dmas * (1 - back))

        def tables_complete(eng, s):
            for b in range(2):
                eng.wait_ge(phases[s].stored[b], 16 * (G // 2))
        def slow_sync(sp):
            sp.wait_ge(zero_set, 1)
            nz = 0
            for t in agg_tab:
                tz = t.rearrange("(c p q) d -> c p (q d)", p=P, q=3584 // D)
                for c in range(tz.shape[0]):
                    sp.dma_start(tz[c], zero[:, :]).then_inc(zeroed, 16)
                    nz += 1
            assert nz == 3 * NP * D // (P * 3584)
            sp.wait_ge(norm_ready, 2)
            sp.dma_start(norm_tab.rearrange("(p c) o -> p (c o)", p=P), nsrc[:, :]).then_inc(tabs_saved, 16)
            sp.wait_ge(deg_saved, 4)
            for c in range(4):
                m = min(P, G * B - c * P)
                sp.dma_start(deg_tab[c * P:c * P + m, :], degT[0:m, c, :]).then_inc(tabs_saved, 16)
            for s in range(3):
                sp.wait_ge(scattered, 16 * ET * (s + 1))
                if s == 2:
                    sp.wait_ge(tabs_saved, 16 * 5)

                def load(g, b, u, s=s):
                    wait(sp, group_out[b], s * (G // 2) + u)
                    sp.dma_start(ga[b][:, :, :], rows_of(agg_tab[s], g)).then_inc(a_in[s][b], 16)
                    if s == 1:
                        if isinstance(g, int) and g == G - 1:
                            sp.dma_start(gx[b][0:LASTP, :, :], x[(G - 1) * GN:N, :].rearrange("(p i) d -> p i d", i=B)).then_inc(x_in[s][b], 16)
                        else:
                            sp.dma_start(gx[b][:, :, :], x[bass.ds(g * GN, GN), :].rearrange("(p i) d -> p i d", i=B)).then_inc(x_in[s][b], 16)
                    if s == 2:
                        sp.dma_start(gx[b][:, :, :], rows_of(x1_tab, g)).then_inc(x_in[s][b], 16)
                        sp.dma_start(gd[b][:, :], deg_tab.rearrange("(g i) p -> g (i p)", i=B)[bass.ds(g, 1), :]).then_inc(d_in[b], 16)
                groups(sp, load)

        def slow_pool(pool):
            nc.gpsimd.memset(zero[:, :], 0.0).then_inc(zero_set, 1)
            pool.wait_ge(zeroed, 16 * 42)
            pool.wait_ge(tabs_saved, 16 * 5)
            feat = [x, hs_tab, x1_tab]
            for s in range(3):
                if s:
                    for b in range(2):
                        pool.wait_ge(stored[s - 1][b], 16 * (G // 2))
                def edges(t, s=s):
                    nc.gpsimd.tensor_copy(col[:, 0:1], src_i[:, bass.ds(t, 1)])
                    nc.gpsimd.tensor_copy(col[:, 1:2], dst_i[:, bass.ds(t, 1)])
                    nc.gpsimd.tensor_copy(col[:, 2:3], nidx_i[:, bass.ds(t, 1)]).then_inc(col_ready, 1)
                    pool.wait_ge(col_ready, t + 1 + s * ET)
                    pool.sem_inc(held, 1)
                    nc.gpsimd.indirect_dma_start(out=rows[:, 0, :], out_offset=None, in_=feat[s][:, :],
                                                 in_offset=bass.IndirectOffsetOnAxis(ap=col[:, 0:1], axis=0)).then_inc(rows_in, 16)
                    if s == 0:
                        nc.gpsimd.indirect_dma_start(out=nrow[:, :], out_offset=None, in_=norm_tab[:, :],
                                                     in_offset=bass.IndirectOffsetOnAxis(ap=col[:, 2:3], axis=0)).then_inc(nrow_in, 16)
                    if s == 2:
                        nc.gpsimd.indirect_dma_start(out=rows[:, 1, :], out_offset=None, in_=feat[s][:, :],
                                                     in_offset=bass.IndirectOffsetOnAxis(ap=col[:, 1:2], axis=0)).then_inc(rows2_in, 16)
                    pool.wait_ge(scat_ready, t + 1 + s * ET)
                    pool.wait_ge(comb_ready, t + 1 + s * ET)
                    pool.sem_inc(held, 1)
                    nc.gpsimd.indirect_dma_start(out=agg_tab[s][:, :], out_offset=bass.IndirectOffsetOnAxis(ap=scat_i[:, 0:1], axis=0),
                                                 in_=comb[:, :], in_offset=None, compute_op=ALU.add).then_inc(scattered, 16)
                    pool.wait_ge(scattered, 16 * t + (16 + s * ET * 16))
                tiles(pool, edges)

        def slow_vector(dve, n, step):
            for k, v in enumerate((src_i, dst_i)):
                step(nc.vector.tensor_scalar(tmp_i[0][:, :], v[:, :], 2, 127, ALU.logical_shift_right, ALU.bitwise_and))
                step(nc.vector.tensor_copy(code[2 * k][:, :], tmp_i[0][:, :]))
                step(nc.vector.tensor_scalar(tmp_i[0][:, :], v[:, :], 9, 2, ALU.logical_shift_right, ALU.logical_shift_left))
                step(nc.vector.tensor_scalar(tmp_i[1][:, :], v[:, :], 3, None, ALU.bitwise_and))
                step(nc.vector.tensor_tensor(code[2 * k + 1][:, :], tmp_i[0][:, :], tmp_i[1][:, :], ALU.add))
            step(nc.vector.scalar_tensor_tensor(nidx_i[:, :], code[0][:, :], float(G * B), code[1][:, :], ALU.mult, ALU.add))
            step(nc.vector.tensor_copy(dst_f[:, :], dst_i[:, :]))
            def hots(b, t, u):
                wait(dve, hist_done, u)
                for k in range(2):
                    nc.vector.tensor_scalar(hot[b][0:EP, k, :], iota_c[0:EP, 0:P], code[2 * k][:, bass.ds(t, 1)], None, ALU.is_equal)
                    last = nc.vector.tensor_scalar(hotc[b][0:EP, k, :], iota_c[0:EP, :], code[2 * k + 1][:, bass.ds(t, 1)], None, ALU.is_equal)
                last.then_inc(hot_ready, 1)
            hots(0, 0, 0)
            hots(1, 1, 0)
            with dve.Fori(1, ET // 2) as i:
                hots(0, 2 * i, i)
                hots(1, 2 * i + 1, i)
            dve.wait_ge(hist_done, ET // 2)
            step(nc.vector.tensor_copy(deg_out[:, :], pA[0][:, 0:G * B]))
            step(nc.vector.tensor_copy(deg_in[:, :], pA[1][:, 0:G * B]))
            for k, (d, r) in enumerate(((deg_out, nsrc), (deg_in, ndst))):
                step(nc.vector.tensor_scalar(rt[:, :], d[:, :], 1.0, None, ALU.max))
                inv = nc.vector.reciprocal(r[:, :], rt[:, :])
                if k == 0:
                    step(inv)
            inv.then_inc(fuse_dve, 1)
            dve.wait_ge(deg_turn, 1)
            for c in range(4):
                m = min(P, G * B - c * P)
                nc.vector.tensor_copy(degT[0:m, c, :], pB[0][0:m, c * P:(c + 1) * P]).then_inc(deg_saved, 1)
            dve.wait_ge(fuse_pe, 1)
            nc.vector.tensor_copy(we2T[:, :], pB[1][:, 0:D]).then_inc(fuse_dve, 1)
            dve.wait_ge(fuse_pe, 2)
            nc.vector.tensor_copy(wf[:, :], pB[1][:, 128:128 + D])
            nc.vector.tensor_copy(vrow[:, :], pB[1][0:1, 256:256 + D]).then_inc(fuse_dve, 1)
            dve.wait_ge(norm_ready, 2)
            for s in range(3):
                def edges(t, s=s, n0=n[0]):
                    wait(dve, comb_ready, t + s * ET)
                    wait(dve, scattered, 16 * t + s * ET * 16)
                    nc.vector.tensor_copy(dstB[:, :], dst_f[:, bass.ds(t, 1)].to_broadcast([EP, EP]))
                    nc.vector.tensor_copy(cnt[:, 2:3], dst_f[:, bass.ds(t, 1)]).then_inc(dst_spread, 1)
                    dve.wait_ge(dst_turned, t + 1 + s * ET)
                    dve.wait_ge(dst_spread, t + 1 + s * ET)
                    nc.vector.tensor_scalar(same[:, :], pA[0][0:EP, 0:EP], cnt[:, 2:3], None, ALU.is_equal).then_inc(same_ready, 1)
                    dve.wait_ge(same_ready, t + 1 + s * ET)
                    nc.vector.tensor_tensor_reduce(out=junk[:, :], in0=same[:, :], in1=lower[0:EP, 0:EP], scale=1.0, scalar=0.0,
                                                   op0=ALU.mult, op1=ALU.add, accum_out=cnt[:, 0:1]).then_inc(chain, 1)
                    dve.wait_ge(chain, t * 4 + (n0 + 1))
                    nc.vector.tensor_scalar(cnt[:, 1:2], cnt[:, 0:1], 0.5, None, ALU.is_lt).then_inc(chain, 1)
                    nc.vector.tensor_tensor(cnt[:, 3:4], cnt[:, 2:3], trash[0:EP, :], ALU.subtract).then_inc(chain, 1)
                    dve.wait_ge(chain, t * 4 + (n0 + 3))
                    nc.vector.tensor_tensor(cnt[:, 0:1], cnt[:, 1:2], cnt[:, 3:4], ALU.mult).then_inc(chain, 1)
                    dve.wait_ge(chain, t * 4 + (n0 + 4))
                    nc.vector.tensor_tensor(scat_i[:, :], cnt[:, 0:1], trash[0:EP, :], ALU.add).then_inc(scat_ready, 1)
                    if s == 0:
                        dve.wait_ge(rows_in, 16 * t + 16)
                        dve.wait_ge(nrow_in, 16 * t + 16)
                        nc.vector.tensor_scalar(msg[:, :], rows[:, 0, :], nrow[:, 0:1], None, ALU.mult).then_inc(msg_ready, 1)
                    if s == 2:
                        dve.wait_ge(edge_mlp, t + 1)
                        nc.vector.tensor_tensor(msg[:, :], pC[0][0:EP, 0:D], be1b[0:EP, :], ALU.add).then_inc(edge_act, 1)
                        dve.wait_ge(edge_act, t + 1)
                        nc.vector.tensor_scalar(msg[:, :], msg[:, :], 0.0, None, ALU.max).then_inc(msg_ready, 1)
                    dve.wait_ge(summed, t + 1 + s * ET)
                    nc.vector.tensor_copy(comb[:, :], pD[0][0:EP, 0:D]).then_inc(comb_ready, 1)
                tiles(dve, edges)
                n[0] += 4 * ET

                def bc(v, g):
                    return v[:, bass.ds(g * B, B)].rearrange("p (i o) -> p i o", o=1).to_broadcast([P, B, D])

                def bd(v):
                    return v[:, :].rearrange("p (o d) -> p o d", o=1).to_broadcast([P, B, D])

                per = {0: 3, 1: 5, 2: 4}[s]
                base = n[0]

                def post(g, b, u, s=s, per=per, base=base):
                    c = [0]

                    def link(ins):
                        c[0] += 1
                        ins.then_inc(chain, 1)
                        dve.wait_ge(chain, g * per + (base + c[0]))

                    def v3(t):
                        return t.rearrange("p (i d) -> p i d", i=B)

                    done = s * G + g
                    if s < 2:
                        dve.wait_ge(mult, done + 1)
                        link(nc.vector.tensor_tensor(y[b][:, :, :], v3(pB[b][:, :]), bc(ndst, g), ALU.mult))
                        link(nc.vector.tensor_tensor(z[b][:, :, :], y[b][:, :, :], bd(b1b if s == 0 else b2b), ALU.add))
                    if s == 0:
                        wait(dve, stored[s][b], 16 * u)
                        link(nc.vector.tensor_scalar(y[b][:, :, :], z[b][:, :, :], 0.0, None, ALU.max))
                        last = nc.vector.tensor_tensor(go[b][:, :, :], y[b][:, :, :], bc(nsrc, g), ALU.mult)
                    else:
                        dve.wait_ge(x_in[s][b], 16 * u + 16)
                        if s == 1:
                            link(nc.vector.scalar_tensor_tensor(y[b][:, :, :], z[b][:, :, :], 0.0, gx[b][:, :, :], ALU.max, ALU.add))
                        else:
                            dve.wait_ge(mult2, g + 1)
                            link(nc.vector.tensor_tensor(z[b][:, :, :], v3(pD[b][:, :]), bd(bn2b), ALU.add))
                            link(nc.vector.scalar_tensor_tensor(y[b][:, :, :], gx[b][:, :, :], 2.0, z[b][:, :, :], ALU.mult, ALU.add))
                        for i in range(B):
                            last = nc.vector.bn_stats(st[:, i, :], y[b][:, i, :])
                        link(last)
                        dve.sem_inc(held_dve, 1)
                        for i in range(B):
                            last = nc.vector.bn_aggr(mv[:, i, :], st[:, i, :])
                        last.then_inc(var_ready, 1)
                        dve.wait_ge(sd_ready, (s - 1) * G + g + 1)
                        link(nc.vector.reciprocal(rs[:, :], sd[:, :]))
                        wait(dve, stored[s][b], 16 * u)
                        for i in range(B):
                            last = nc.vector.tensor_scalar(go[b][:, i, :], y[b][:, i, :], mv[:, i, 0:1], rs[:, i:i + 1], ALU.subtract, ALU.mult)
                    assert c[0] == per
                    last.then_inc(group_out[b], 1)
                groups(dve, post)
                n[0] += per * G

        def slow_scalar(act):
            act.wait_ge(fuse_dve, 1)
            nc.scalar.activation(nsrc[:, :], nsrc[:, :], ACT.Sqrt).then_inc(norm_ready, 1)
            nc.scalar.activation(ndst[:, :], ndst[:, :], ACT.Sqrt).then_inc(norm_ready, 1)
            for s in range(3):
                if s:
                    act.wait_ge(loaded, 16 * LOADS)
                if s == 2:
                    def edges(t):
                        act.wait_ge(edge_turned, t + 1)
                        nc.scalar.copy(edT[:, :, :], pB[0][:, 0:2 * EP].rearrange("p (k e) -> p k e", k=2)).then_inc(edge_copied, 1)
                    tiles(act, edges)

                def pre(g, b, u, s=s):
                    act.wait_ge(turned, s * G + g + 1)
                    nc.scalar.copy(aT[b][:, :], pA[b][:, :]).then_inc(copied, 1)
                    if s == 2:
                        nc.scalar.copy(xT[b][:, :], pC[b][:, :]).then_inc(copied, 1)
                        act.wait_ge(mult, s * G + g + 1)
                        nc.scalar.activation(mT[b][:, :], pB[b][:, :], ACT.Relu, bias=bn1c[:, 0:1]).then_inc(hidden, 1)
                    if s:
                        act.wait_ge(var_ready, (s - 1) * G + g + 1)
                        nc.scalar.activation(sd[:, :], mv[:, :, 1], ACT.Sqrt, bias=eps[:, 0:1]).then_inc(sd_ready, 1)
                    act.wait_ge(group_out[b], s * (G // 2) + u + 1)
                    if s < 2:
                        act.dma_start(rows_of(hs_tab if s == 0 else x1_tab, g), go[b][:, :, :]).then_inc(stored[s][b], 16)
                    elif isinstance(g, int) and g == G - 1:
                        act.dma_start(out[(G - 1) * GN:N, :].rearrange("(p i) d -> p i d", i=B), go[b][0:LASTP, :, :]).then_inc(stored[s][b], 16)
                    else:
                        act.dma_start(out[bass.ds(g * GN, GN), :].rearrange("(p i) d -> p i d", i=B), go[b][:, :, :]).then_inc(stored[s][b], 16)
                groups(act, pre)
            for b in range(2):
                act.wait_ge(stored[2][b], 16 * (G // 2))

        def slow_tensor(pe):
            def hist(b, t, i, start=False, stop=False):
                pe.wait_ge(hot_ready, t + 1)
                for k in range(2):
                    last = nc.tensor.matmul(pA[k][:, 0:G * B], hot[b][0:EP, k, :], hotc[b][0:EP, k, :], start=start, stop=stop)
                return last
            hist(0, 0, 0, start=True)
            hist(1, 1, 0).then_inc(hist_done, 1)
            with pe.Fori(1, ET // 2 - 1) as i:
                hist(0, 2 * i, i)
                hist(1, 2 * i + 1, i).then_inc(hist_done, 1)
            hist(0, ET - 2, 0)
            hist(1, ET - 1, 0, stop=True).then_inc(hist_done, 1)
            pe.wait_ge(fuse_dve, 1)
            for c in range(4):
                m = min(P, G * B - c * P)
                last = nc.tensor.transpose(pB[0][0:m, c * P:(c + 1) * P], deg_in[:, c * P:c * P + m], ident[:, :])
            last.then_inc(deg_turn, 1)
            nc.tensor.transpose(pB[1][:, 0:D], we2[:, :], ident[:, :]).then_inc(fuse_pe, 1)
            pe.wait_ge(fuse_dve, 2)
            nc.tensor.matmul(pB[1][:, 128:128 + D], we2T[:, :], wn1b[:, :], start=True, stop=True)
            nc.tensor.matmul(pB[1][0:1, 256:256 + D], be2c[:, :], wn1b[:, :], start=True, stop=True).then_inc(fuse_pe, 1)
            pe.wait_ge(fuse_dve, 3)
            pe.wait_ge(deg_saved, 4)
            for s in range(3):
                def edges(t, s=s):
                    pe.wait_ge(dst_spread, t + 1 + s * ET)
                    nc.tensor.transpose(pA[0][0:EP, 0:EP], dstB[:, :], ident[0:EP, 0:EP]).then_inc(dst_turned, 1)
                    if s == 2:
                        pe.wait_ge(rows_in, 16 * t + (16 + s * ET * 16))
                        pe.wait_ge(rows2_in, 16 * t + 16)
                        for k in range(2):
                            last = nc.tensor.transpose(pB[0][:, k * EP:(k + 1) * EP], rows[:, k, :], ident[0:EP, 0:EP])
                        last.then_inc(edge_turned, 1)
                        pe.wait_ge(edge_copied, t + 1)
                        nc.tensor.matmul(pC[0][0:EP, 0:D], edT[:, 0, :], we1a[:, :], start=True, stop=False)
                        nc.tensor.matmul(pC[0][0:EP, 0:D], edT[:, 1, :], we1b[:, :], start=False, stop=True).then_inc(edge_mlp, 1)
                    pe.wait_ge(same_ready, t + 1 + s * ET)
                    if s == 1:
                        pe.wait_ge(rows_in, 16 * t + (16 + s * ET * 16))
                        m = rows[:, 0, :]
                    else:
                        pe.wait_ge(msg_ready, t + 1 + (ET if s == 2 else 0))
                        m = msg[:, :]
                    nc.tensor.matmul(pD[0][0:EP, 0:D], same[:, :], m, start=True, stop=True).then_inc(summed, 1)
                tiles(pe, edges)

                def mm(g, b, u, s=s):
                    wait(pe, group_out[b], s * (G // 2) + u)
                    pe.wait_ge(a_in[s][b], 16 * u + 16)
                    if s == 2:
                        pe.wait_ge(x_in[s][b], 16 * u + 16)
                    for i in range(B):
                        last = nc.tensor.transpose(pA[b][:, i * P:(i + 1) * P], ga[b][:, i, :], ident[:, :])
                        if s == 2:
                            last = nc.tensor.transpose(pC[b][:, i * P:(i + 1) * P], gx[b][:, i, :], ident[:, :])
                    last.then_inc(turned, 1)
                    if s < 2:
                        pe.wait_ge(copied, s * G + g + 1)
                        for i in range(B):
                            last = nc.tensor.matmul(pB[b][:, i * P:(i + 1) * P], aT[b][:, i * P:(i + 1) * P],
                                                    (w1 if s == 0 else w2)[:, :], start=True, stop=True)
                        last.then_inc(mult, 1)
                    else:
                        pe.wait_ge(copied, 2 * g + (2 * G + 2))
                        nc.tensor.matmul(pB[b][:, :], wn1a[:, :], xT[b][:, :], start=True, stop=False)
                        nc.tensor.matmul(pB[b][:, :], wf[:, :], aT[b][:, :], start=False, stop=False)
                        pe.wait_ge(d_in[b], 16 * u + 16)
                        nc.tensor.matmul(pB[b][:, :], vrow[:, :], gd[b][:, :], start=False, stop=True).then_inc(mult, 1)
                        pe.wait_ge(hidden, g + 1)
                        for i in range(B):
                            last = nc.tensor.matmul(pD[b][:, i * P:(i + 1) * P], mT[b][:, i * P:(i + 1) * P], wn2[:, :], start=True, stop=True)
                        last.then_inc(mult2, 1)
                groups(pe, mm)

        def fast_sync(sp):
            sp.wait_ge(f_norm, 2)
            sp.dma_start(norm_tab.rearrange("(p c) o -> p (c o)", p=P), nsrc[:, :]).then_inc(f_tabs, 16)
            sp.wait_ge(f_deg16, 4)
            for c in range(4):
                m = min(P, G * B - c * P)
                sp.dma_start(deg16_tab[c * P:c * P + m, :], degT16[0:m, c, :]).then_inc(f_tabs, 16)
            sp.wait_ge(f_parts, 1)
            sp.dma_start(vpart_tab.rearrange("(o k) d -> o k d", o=1), vparts[:, :, :]).then_inc(f_parts_in, 16)
            sp.wait_ge(f_parts_in, 16)
            sp.dma_start(vp3[:, :, :], vpart_tab.rearrange("(k v) d -> k v d", v=2)).then_inc(f_parts_in, 16)
            for s in range(3):
                ph = phases[s]
                if s:
                    tables_complete(sp, s - 1)
                if s == 2:
                    sp.wait_ge(f_tabs, 16 * 5)

                lag = (3, 3, 4)[s]

                def body(at, s=s, ph=ph, lag=lag):
                    g = at(0)
                    if g:
                        if s == 0:
                            after(sp, ph.hot_set, g, 4)
                        else:
                            after(sp, ph.posted, g, 4)
                            after(sp, ph.hid if s == 2 else ph.summed, g, 4)
                        sp.sem_inc(held, 1)
                        last = isinstance(g.g, int) and g.g == G - 1
                        for t, tab, arrived in ((fx, (x, hs_tab, x1_tab)[s], ph.x_in), (fx2, x, ph.x2_in)):
                            if t is fx2 and s != 1:
                                continue
                            if tab is x and last:
                                sp.dma_start(t[g.r][0:LASTP, :, :], x[(G - 1) * GN:N, :].rearrange("(p i) d -> p i d", i=B)).then_inc(arrived[g.r], 16)
                            else:
                                sp.dma_start(t[g.r][:, :, :], tab[bass.ds(g.g * GN, GN), :].rearrange("(p i) d -> p i d", i=B)).then_inc(arrived[g.r], 16)
                        if s == 2:
                            sp.dma_start(fd[g.r][:, :], deg16_tab.rearrange("(g i) p -> g (i p)", i=B)[bass.ds(g.g, 1), :].to_broadcast([3, GN])).then_inc(ph.d_in[g.r], 16)
                    g = at(-lag)
                    if g:
                        after(sp, ph.result, g)
                        sp.sem_inc(held, 1)
                        if s < 2:
                            sp.dma_start((hs_tab, x1_tab)[s][bass.ds(g.g * GN, GN), :].rearrange("(p i) d -> p i d", i=B), go[g.b][:, :, :]).then_inc(ph.stored[g.b], 16)
                        elif isinstance(g.g, int) and g.g == G - 1:
                            sp.dma_start(out[(G - 1) * GN:N, :].rearrange("(p i) d -> p i d", i=B), go[g.b][0:LASTP, :, :]).then_inc(ph.stored[g.b], 16)
                        else:
                            sp.dma_start(out[bass.ds(g.g * GN, GN), :].rearrange("(p i) d -> p i d", i=B), go[g.b][:, :, :]).then_inc(ph.stored[g.b], 16)
                pipeline(sp, body, 0, lag)
            tables_complete(sp, 2)

        def fast_pool(pool):
            for r in range(4):
                nc.gpsimd.memset(fr[r][:, :, :], 0.0).then_inc(f_clean, 1)
                nc.gpsimd.memset(fn[r][:, :], 0.0).then_inc(f_clean, 1)
            pool.wait_ge(f_clean, 8)
            pool.wait_ge(slots_set, 1)
            pool.wait_ge(f_tabs, 16 * 5)
            for s in range(3):
                ph = phases[s]
                if s:
                    tables_complete(pool, s - 1)
                n_rows = 2 if s == 1 else 4

                def body(at, s=s, ph=ph, n_rows=n_rows):
                    g = at(1)
                    if g:
                        landed(pool, ph.gathered, g, n_rows, 1)
                        last = nc.gpsimd.tensor_copy(fcol[g.r][:, 0:2], sidx[:, :, bass.ds(g.g, 1)].rearrange("p h o -> p (h o)"))
                        if s != 1:
                            last = nc.gpsimd.tensor_copy(fcol[g.r][:, 2:4], (nidx, None, didx)[s][:, :, bass.ds(g.g, 1)].rearrange("p h o -> p (h o)"))
                        last.then_inc(ph.col_set, 1)
                    g = at(0)
                    if g:
                        after(pool, ph.col_set, g)
                        after(pool, ph.summed, g, 4)
                        if s == 0:
                            after(pool, ph.hot_set, g, 4)
                        pool.sem_inc(held, 1)
                        for k in range(n_rows):
                            if s == 0 and k > 1:
                                dest, tab, bound = fn[g.r][:, k - 2:k - 1], norm_tab, P * G * B - 1
                            else:
                                dest, tab, bound = fr[g.r][:, k, :], (x, hs_tab, x1_tab)[s], N - 1
                            nc.gpsimd.indirect_dma_start(out=dest, out_offset=None, in_=tab[:, :],
                                                         in_offset=bass.IndirectOffsetOnAxis(ap=fcol[g.r][:, k:k + 1], axis=0),
                                                         bounds_check=bound, oob_is_err=False).then_inc(ph.gathered[g.r], 16)
                pipeline(pool, body, 1, 0)

        def fast_vector(dve, n):
            def step(ins):
                n[0] += 1
                ins.then_inc(chain, 1)
                dve.wait_ge(chain, n[0])

            for k in range(SLOTS // 8):
                for h in range(2):
                    last = nc.vector.max(keys[0:G, h, 8 * k:8 * k + 8], wa[0:G, h, :])
                step(last)
                if k < SLOTS // 8 - 1:
                    for h in range(2):
                        last = nc.vector.match_replace(wa[0:G, h, :], keys[0:G, h, 8 * k:8 * k + 8], wa[0:G, h, :], -1.0)
                    step(last)
            dve.sem_inc(keys_set, 1)
            dve.wait_ge(keys_turned, 1)
            step(nc.vector.tensor_copy(kT[:, :, :], pA[0][:, 0:T].rearrange("p (h g) -> p h g", h=2)))

            def bits(dest, of, a, b, opa, opb=None):
                step(nc.vector.tensor_scalar(dest[:, :, :], of[:, :, :], a, b, opa, opb) if opb is not None
                     else nc.vector.tensor_scalar(dest[:, :, :], of[:, :, :], a, None, opa))
            SHR, SHL, AND = ALU.logical_shift_right, ALU.logical_shift_left, ALU.bitwise_and
            bits(sidx, kT, KEY - 1, None, AND)
            bits(t0, kT, 16, None, SHR)
            step(nc.vector.tensor_tensor(didx[:, :, :], t0[:, :, :], tile_first[:, :, :], ALU.add))
            bits(t1, t0, 3, None, AND)
            step(nc.vector.tensor_copy(di[:, :, :], t1[:, :, :]))
            bits(t2, t0, 2, None, SHR)
            step(nc.vector.tensor_copy(dq[:, :, :], t2[:, :, :]))
            step(nc.vector.scalar_tensor_tensor(dcode[:, :, :], t1[:, :, :], 64.0, t2[:, :, :], ALU.mult, ALU.add))
            bits(t0, sidx, 2, P - 1, SHR, AND)
            step(nc.vector.tensor_copy(srow[:, :, :], t0[:, :, :]))
            bits(t1, sidx, 9, 2, SHR, SHL)
            bits(t2, sidx, 3, None, AND)
            step(nc.vector.tensor_tensor(scol[:, :, :], t1[:, :, :], t2[:, :, :], ALU.add))
            step(nc.vector.scalar_tensor_tensor(nidx[:, :, :], srow[:, :, :], float(G * B), scol[:, :, :], ALU.mult, ALU.add))
            dve.sem_inc(slots_set, 1)
            def hots(t, b, u):
                wait(dve, f_hist, t - 1)
                nc.vector.tensor_scalar(hot[b][:, 0, :], iota_b[:, 0:P], srow[:, :, :].rearrange("p h g -> p (h g)")[:, bass.ds(t, 1)], None, ALU.is_equal)
                nc.vector.tensor_scalar(hotc[b][:, 0, :], iota_c[:, :], scol[:, :, :].rearrange("p h g -> p (h g)")[:, bass.ds(t, 1)], None, ALU.is_equal).then_inc(f_hot, 1)
            hots(0, 0, 0)
            hots(1, 1, 0)
            with dve.Fori(1, T // 2) as i:
                hots(2 * i, 0, i)
                hots(2 * i + 1, 1, i)
            for h in range(2):
                if h:
                    dve.wait_ge(f_in, 1)
                step(nc.vector.tensor_tensor(hp[:, :, :], iota_b[:, 0:64].rearrange("p (o q) -> p o q", o=1).to_broadcast([P, G, 64]),
                                             dq[:, h, :].rearrange("p (g o) -> p g o", o=1).to_broadcast([P, G, 64]), ALU.is_equal))
                nc.vector.tensor_tensor(hi[:, :, :], iota_b[:, 0:B].rearrange("p (o q) -> p o q", o=1).to_broadcast([P, G, B]),
                                        di[:, h, :].rearrange("p (g o) -> p g o", o=1).to_broadcast([P, G, B]), ALU.is_equal).then_inc(f_hp, 1)
            dve.wait_ge(f_hist, T)
            dve.wait_ge(f_in, 2)
            step(nc.vector.tensor_scalar(deg_out[:, :], pA[1][:, 0:G * B], 1.0, None, ALU.add))
            step(nc.vector.tensor_scalar(deg_in[:, :], pD[0][:, 0:G * B], 1.0, None, ALU.add))
            nc.vector.reciprocal(nsrc[:, :], deg_out[:, :])
            nc.vector.reciprocal(ndst[:, :], deg_in[:, :]).then_inc(f_recip, 1)
            dve.wait_ge(f_degt, 1)
            for c in range(4):
                m = min(P, G * B - c * P)
                nc.vector.tensor_copy(degT16[0:m, c, :], pB[0][0:m, c * P:(c + 1) * P]).then_inc(f_deg16, 1)
            dve.wait_ge(f_fuse_pe, 1)
            nc.vector.tensor_copy(we2T[:, :], pB[1][:, 0:D])
            nc.vector.tensor_tensor(wes[:, :], we1a[:, :], we1b[:, :], ALU.add).then_inc(f_fuse, 1)
            dve.wait_ge(f_fuse_pe, 2)
            nc.vector.tensor_copy(wf[:, :], pB[1][:, 128:128 + D])
            step(nc.vector.tensor_copy(vrow[:, :], pB[1][0:1, 256:256 + D]))
            for v, row in enumerate((vrow, be1r)):
                step(nc.vector.tensor_copy(vparts[:, 0 + v, :], row[:, :]))
                step(nc.vector.tensor_tensor(vres[:, 0, :], row[:, :], vparts[:, 0 + v, :], ALU.subtract))
                step(nc.vector.tensor_copy(vparts[:, 2 + v, :], vres[:, 0, :]))
                step(nc.vector.tensor_tensor(vres[:, 1, :], vres[:, 0, :], vparts[:, 2 + v, :], ALU.subtract))
                step(nc.vector.tensor_copy(vparts[:, 4 + v, :], vres[:, 1, :]))
            dve.sem_inc(f_parts, 1)
            dve.wait_ge(f_norm, 2)

            def per_group(v, g):
                return v[:, bass.ds(g.g * B, B)].rearrange("p (i o) -> p i o", o=1).to_broadcast([P, B, D])

            def bias(v):
                return v[:, :].rearrange("p (o d) -> p o d", o=1).to_broadcast([P, B, D])

            def v3(t):
                return t.rearrange("p (i d) -> p i d", i=B)

            for s in range(3):
                ph = phases[s]
                if s:
                    tables_complete(dve, s - 1)
                per = (1, 3, 3)[s]
                base = n[0]

                def hot_rows(g, s=s, ph=ph):
                    after(dve, ph.summed if s < 2 else ph.rsum, g, 2)
                    if s == 0:
                        dve.wait_ge(ph.x_in[g.r], 16 * g.u + 16)
                        nc.vector.tensor_tensor(y[g.b][:, :, :], fx[g.r][:, :, :], per_group(nsrc, g), ALU.mult)
                        landed(dve, ph.gathered, g, 4)
                    for h in range(2):
                        c = dcode[:, h, bass.ds(g.g, 1)]
                        if s == 0:
                            last = nc.vector.tensor_scalar(fhot[g.b][:, h, :], iota_b[:, :], c, fn[g.r][:, h:h + 1], ALU.is_equal, ALU.mult)
                        else:
                            last = nc.vector.tensor_scalar(fhot[g.b][:, h, :], iota_b[:, :], c, None, ALU.is_equal)
                    last.then_inc(ph.hot_set, 1)

                def link(g, k, ins, per=per, base=base):
                    ins.then_inc(chain, 1)
                    dve.wait_ge(chain, g.g * per + (base + k))

                def post(g, s=s, ph=ph, link=link):
                    if s == 0:
                        after(dve, ph.scaled, g)
                        link(g, 1, nc.vector.tensor_tensor(z[g.b][:, :, :], z[g.b][:, :, :], bias(b1b), ALU.add))
                        wait(dve, ph.stored[g.b], 16 * g.half)
                        nc.vector.scalar_tensor_tensor(go[g.b][:, :, :], z[g.b][:, :, :], 0.0, per_group(nsrc, g), ALU.max, ALU.mult).then_inc(ph.result, 1)
                        return
                    if s == 1:
                        after(dve, ph.scaled, g)
                        dve.wait_ge(ph.x2_in[g.r], 16 * g.u + 16)
                        link(g, 1, nc.vector.tensor_tensor(z[g.b][:, :, :], z[g.b][:, :, :], bias(b2b), ALU.add))
                        after(dve, ph.result, g, 4)
                        link(g, 2, nc.vector.scalar_tensor_tensor(fy[g.r][:, :, :], z[g.b][:, :, :], 0.0, fx2[g.r][:, :, :], ALU.max, ALU.add))
                    else:
                        after(dve, ph.outp, g)
                        link(g, 1, nc.vector.tensor_tensor(z[g.b][:, :, :], v3(pD[g.b][:, :]), bias(bn2b), ALU.add))
                        after(dve, ph.result, g, 4)
                        link(g, 2, nc.vector.scalar_tensor_tensor(fy[g.r][:, :, :], fx[g.r][:, :, :], 2.0, z[g.b][:, :, :], ALU.mult, ALU.add))
                    for i in range(B):
                        last = nc.vector.bn_stats(fst[g.r][:, i, :], fy[g.r][:, i, :])
                    link(g, 3, last)
                    dve.sem_inc(held_dve, 1)
                    for i in range(B):
                        last = nc.vector.bn_aggr(fmv[g.r][:, i, :], fst[g.r][:, i, :])
                    last.then_inc(ph.posted, 1)

                def invert(g, ph=ph):
                    after(dve, ph.rooted, g)
                    nc.vector.reciprocal(frs[g.r][:, :], fsd[g.r][:, :]).then_inc(ph.recip, 1)
                    after(dve, ph.recip, g)
                    nc.vector.scalar_tensor_tensor(fnm[g.r][:, :], fmv[g.r][:, :, 0], -1.0, frs[g.r][:, :], ALU.mult, ALU.mult).then_inc(ph.inverted, 1)

                def body(at, s=s, ph=ph):
                    if s == 2 and at(0):
                        g = at(0)
                        after(dve, ph.rsum, g)
                        after(dve, ph.scaled, g)
                        after(dve, ph.hid, g, 2)
                        nc.vector.tensor_tensor(aT[g.b][:, :], pC[0][:, :], fs[g.b][:, :], ALU.add).then_inc(ph.radd, 1)
                    if at(1 if s < 2 else 2):
                        hot_rows(at(1 if s < 2 else 2))
                    if at(0 if s < 2 else -1):
                        post(at(0 if s < 2 else -1))
                    if s and at(-1 if s < 2 else -2):
                        invert(at(-1 if s < 2 else -2))
                pipeline(dve, body, 2 if s == 2 else 1, (0, 1, 2)[s])
                n[0] += per * G

        def fast_scalar(act):
            act.wait_ge(f_recip, 1)
            nc.scalar.activation(nsrc[:, :], nsrc[:, :], ACT.Sqrt).then_inc(f_norm, 1)
            nc.scalar.activation(ndst[:, :], ndst[:, :], ACT.Sqrt).then_inc(f_norm, 1)
            act.wait_ge(f_norm, 2)
            act.wait_ge(loaded, 16 * LOADS)
            for s in range(3):
                ph = phases[s]
                if s:
                    tables_complete(act, s - 1)

                def normalise(g, ph=ph):
                    after(act, ph.inverted, g)
                    wait(act, ph.stored[g.b], 16 * g.half)
                    for i in range(B):
                        last = nc.scalar.activation(go[g.b][:, i, :], fy[g.r][:, i, :], ACT.Identity,
                                                    scale=frs[g.r][:, i:i + 1], bias=fnm[g.r][:, i:i + 1])
                    last.then_inc(ph.result, 1)

                def root(g, ph=ph):
                    after(act, ph.posted, g)
                    nc.scalar.activation(fsd[g.r][:, :], fmv[g.r][:, :, 1], ACT.Sqrt, bias=eps[:, 0:1]).then_inc(ph.rooted, 1)

                def body(at, s=s, ph=ph, root=root, normalise=normalise):
                    g = at(1)
                    if g:
                        after(act, ph.summed, g)
                        if s < 2:
                            after(act, ph.mixed, g, 2)
                            nc.scalar.copy(aT[g.b][:, :], pA[g.b][:, :]).then_inc(ph.evacuated, 1)
                        else:
                            after(act, ph.hid, g, 2)
                            nc.scalar.copy(xT[g.b][:, :], pA[0][:, :])
                            nc.scalar.copy(fe[g.b][:, :], pA[1][:, :]).then_inc(ph.evacuated, 1)
                    if s == 2:
                        if at(-2):
                            root(at(-2))
                        if at(-3):
                            normalise(at(-3))
                        g = at(1)
                        if g:
                            after(act, ph.mixed, g)
                            after(act, ph.rsum, g, 2)
                            nc.scalar.activation(fm[g.b][:, :, :], pB[1][:, 0:2 * D].rearrange("p (h d) -> p h d", h=2), ACT.Relu)
                            after(act, ph.radd, g, 2)
                            nc.scalar.activation(fs[g.b][:, :], pB[0][:, :], ACT.Relu, bias=be1c[:, 0:1]).then_inc(ph.scaled, 1)
                        g = at(0)
                        if g:
                            after(act, ph.hid, g)
                            after(act, ph.outp, g, 2)
                            nc.scalar.activation(mT[g.b][:, :], pC[1][:, :], ACT.Relu, bias=bn1c[:, 0:1]).then_inc(ph.hidact, 1)
                        return
                    g = at(0)
                    if g:
                        after(act, ph.mixed, g)
                        after(act, ph.result if s == 0 else ph.posted, g, 2)
                        for i in range(B):
                            last = nc.scalar.activation(z[g.b][:, i, :], pB[g.b][:, i * D:(i + 1) * D], ACT.Identity,
                                                        scale=ndst[:, bass.ds(g.g * B + i, 1)])
                        last.then_inc(ph.scaled, 1)
                    if s == 1:
                        if at(-1):
                            root(at(-1))
                        if at(-2):
                            normalise(at(-2))
                pipeline(act, body, 1, (0, 2, 3)[s])

        def fast_tensor(pe):
            pe.wait_ge(keys_set, 1)
            for h in range(2):
                last = nc.tensor.transpose(pA[0][:, h * G:(h + 1) * G], keys[0:G, h, :], ident[0:G, 0:G])
            last.then_inc(keys_turned, 1)
            def hist(t, b, start=False, stop=False):
                pe.wait_ge(f_hot, t + 1)
                nc.tensor.matmul(pA[1][:, 0:G * B], hot[b][:, 0, :], hotc[b][:, 0, :], start=start, stop=stop).then_inc(f_hist, 1)
            hist(0, 0, start=True)
            hist(1, 1)
            with pe.Fori(1, T // 2 - 1) as i:
                hist(2 * i, 0)
                hist(2 * i + 1, 1)
            hist(T - 2, 0)
            hist(T - 1, 1, stop=True)
            for h in range(2):
                pe.wait_ge(f_hp, h + 1)
                for g in range(G):
                    last = nc.tensor.matmul(pD[0][64 * h:64 * h + 64, B * g:B * g + B], hp[:, g, :], hi[:, g, :], start=True, stop=True)
                last.then_inc(f_in, 1)
            pe.wait_ge(f_recip, 1)
            for c in range(4):
                m = min(P, G * B - c * P)
                last = nc.tensor.transpose(pB[0][0:m, c * P:(c + 1) * P], deg_in[:, c * P:c * P + m], ident[:, :])
            last.then_inc(f_degt, 1)
            nc.tensor.transpose(pB[1][:, 0:D], we2[:, :], ident[:, :]).then_inc(f_fuse_pe, 1)
            pe.wait_ge(f_fuse, 1)
            nc.tensor.matmul(pB[1][:, 128:128 + D], we2T[:, :], wn1b[:, :], start=True, stop=True)
            nc.tensor.matmul(pB[1][0:1, 256:256 + D], be2c[:, :], wn1b[:, :], start=True, stop=True).then_inc(f_fuse_pe, 1)
            pe.wait_ge(f_parts, 1)
            pe.wait_ge(f_parts_in, 32)
            pe.wait_ge(f_deg16, 4)

            def halves(t, h):
                return t[:, :].rearrange("p (i h q) -> p h i q", i=B, h=2)[:, h]

            for s in range(3):
                ph = phases[s]
                if s:
                    tables_complete(pe, s - 1)

                def sums(dest, rows, g, first):
                    for h in range(2):
                        last = nc.tensor.matmul(halves(dest, h), rows[:, h, :], fhot[g.b][:, h, :].rearrange("p (i q) -> p i q", i=B),
                                                start=first and h == 0, stop=h == 1, skip_group_check=True)
                    return last

                def stage_a(g, s=s, ph=ph, sums=sums):
                    if s < 2:
                        after(pe, ph.hot_set, g)
                        pe.wait_ge(ph.x_in[g.r], 16 * g.u + 16)
                        landed(pe, ph.gathered, g, 4 if s == 0 else 2)
                        after(pe, ph.evacuated, g, 2)
                        for i in range(B):
                            nc.tensor.matmul(pA[g.b][:, i * P:(i + 1) * P], (y[g.b] if s == 0 else fx[g.r])[:, i, :], ident[:, :],
                                             start=i == 0, stop=False, skip_group_check=True)
                        sums(pA[g.b], fr[g.r], g, False).then_inc(ph.summed, 1)
                        return
                    pe.wait_ge(ph.x_in[g.r], 16 * g.u + 16)
                    landed(pe, ph.gathered, g, 4)
                    after(pe, ph.evacuated, g, 1)
                    for i in range(B):
                        nc.tensor.transpose(pA[0][:, i * P:(i + 1) * P], fx[g.r][:, i, :], ident[:, :])
                        last = nc.tensor.transpose(pA[1][:, i * P:(i + 1) * P], fr[g.r][:, i, :], ident[:, :])
                    last.then_inc(ph.summed, 1)

                def stage_b(g, s=s, ph=ph):
                    after(pe, ph.evacuated, g)
                    if s < 2:
                        after(pe, ph.scaled, g, 2)
                        for i in range(B):
                            last = nc.tensor.matmul(pB[g.b][:, i * P:(i + 1) * P], aT[g.b][:, i * P:(i + 1) * P],
                                                    (w1 if s == 0 else w2)[:, :], start=True, stop=True)
                        last.then_inc(ph.mixed, 1)
                        return
                    after(pe, ph.scaled, g, 1)
                    nc.tensor.matmul(pB[0][:, :], wes[:, :], xT[g.b][:, :], start=True, stop=True)
                    for h in range(2):
                        m = pB[1][:, h * D:(h + 1) * D]
                        nc.tensor.matmul(m, onesb[0:3, :], vp3[:, 1, :], start=True, stop=False)
                        nc.tensor.matmul(m, fe[g.b][:, h * P:(h + 1) * P], we1a[:, :], start=False, stop=False)
                        last = nc.tensor.matmul(m, fe[g.b][:, (2 + h) * P:(3 + h) * P], we1b[:, :], start=False, stop=True)
                    last.then_inc(ph.mixed, 1)

                def body(at, s=s, ph=ph, stage_a=stage_a, stage_b=stage_b, sums=sums):
                    if at(1):
                        stage_a(at(1))
                    if s < 2:
                        if at(0):
                            stage_b(at(0))
                        return
                    g = at(0)
                    if g:
                        after(pe, ph.hot_set, g)
                        after(pe, ph.scaled, g)
                        after(pe, ph.radd, g, 1)
                        sums(pC[0], fm[g.b], g, True).then_inc(ph.rsum, 1)
                    g = at(-1)
                    if g:
                        after(pe, ph.hidact, g)
                        after(pe, ph.posted, g, 2)
                        for i in range(B):
                            last = nc.tensor.matmul(pD[g.b][:, i * P:(i + 1) * P], mT[g.b][:, i * P:(i + 1) * P], wn2[:, :], start=True, stop=True)
                        last.then_inc(ph.outp, 1)
                    if at(1):
                        stage_b(at(1))
                    g = at(0)
                    if g:
                        nc.tensor.matmul(pC[1][:, :], wn1a[:, :], xT[g.b][:, :], start=True, stop=False)
                        after(pe, ph.radd, g)
                        nc.tensor.matmul(pC[1][:, :], wf[:, :], aT[g.b][:, :], start=False, stop=False)
                        pe.wait_ge(ph.d_in[g.r], 16 * g.u + 16)
                        nc.tensor.matmul(pC[1][:, :], vp3[:, 0, :], fd[g.r][:, :], start=False, stop=True).then_inc(ph.hid, 1)
                pipeline(pe, body, 1, 1 if s == 2 else 0)
        block = ctx.enter_context(nc.Block())

        @block.sync
        def _(sp):
            sp.dma_start(src_i[:, :], src.rearrange("(p t) -> p t", p=EP)).then_inc(loaded, 16)
            sp.dma_start(dst_i[:, :], dst.rearrange("(p t) -> p t", p=EP)).then_inc(loaded, 16)
            for w, a in ((w1, W1), (w2, W2), (we1a, We1[0:P, :]), (we1b, We1[P:2 * P, :]), (we2, We2),
                         (wn1a, Wn1[0:P, :]), (wn1b, Wn1[P:2 * P, :]), (wn2, Wn2)):
                sp.dma_start(w[:, :], a).then_inc(loaded, 16)
            with nc.allow_non_contiguous_dma(reason="bias columns"):
                sp.dma_start(be2c[:, :], be2.rearrange("(p o) -> p o", o=1)).then_inc(loaded, 16)
                sp.dma_start(bn1c[:, :], bn1.rearrange("(p o) -> p o", o=1)).then_inc(loaded, 16)
            for w, a in ((b1b, b1), (b2b, b2), (be1b, be1), (bn2b, bn2)):
                sp.dma_start(w[:, :], a.rearrange("(o d) -> o d", o=1).to_broadcast([P, D])).then_inc(loaded, 16)
            with nc.allow_non_contiguous_dma(reason="bias columns"):
                sp.dma_start(be1c[:, :], be1.rearrange("(p o) -> p o", o=1)).then_inc(loaded, 16)
            sp.dma_start(be1r[:, :], be1.rearrange("(o d) -> o d", o=1)).then_inc(loaded, 16)
            sp.wait_ge(verdict_set, 1)
            regular = sp.value_load(regular_i[0:1, 0:1], min_val=0, max_val=1)
            with sp.If(regular == 1):
                fast_sync(sp)
            with sp.Else():
                slow_sync(sp)

        @block.gpsimd
        def _(pool):
            nc.gpsimd.memset(ones[:, :], 1.0).then_inc(consts, 1)
            nc.gpsimd.memset(eps[:, :], EPS).then_inc(consts, 1)
            nc.gpsimd.iota(iota_c[:, :], [[1, G * B]], base=0, channel_multiplier=0, allow_small_or_imprecise_dtypes=True).then_inc(consts, 1)
            nc.gpsimd.iota(iota_p[:, :], [[0, 1]], base=0, channel_multiplier=1, allow_small_or_imprecise_dtypes=True).then_inc(consts, 1)
            nc.gpsimd.iota(trash[:, :], [[0, 1]], base=TRASH, channel_multiplier=1, allow_small_or_imprecise_dtypes=True).then_inc(consts, 1)
            pool.wait_ge(consts, 5)
            nc.gpsimd.affine_select(out=ident[:, :], in_=ones[:, :], compare_op=ALU.is_equal, fill=0.0,
                                    base=0, pattern=[[-1, P]], channel_multiplier=1).then_inc(consts, 1)
            nc.gpsimd.affine_select(out=lower[:, :], in_=ones[:, :], compare_op=ALU.is_gt, fill=0.0,
                                    base=0, pattern=[[-1, P]], channel_multiplier=1).then_inc(consts, 1)
            nc.gpsimd.affine_select(out=upper[:, :], in_=ones[:, :], compare_op=ALU.is_gt, fill=0.0,
                                    base=0, pattern=[[1, P]], channel_multiplier=-1).then_inc(consts, 1)
            nc.gpsimd.memset(onesb[:, :], 1.0).then_inc(consts, 1)
            nc.gpsimd.memset(check[:, :], 0.0).then_inc(consts, 1)
            nc.gpsimd.iota(tile_first[:, :, :], [[HN, 2], [GN, G]], base=0, channel_multiplier=0, allow_small_or_imprecise_dtypes=True).then_inc(consts, 1)
            nc.gpsimd.iota(my_first[:, :], [[HN, 2]], base=0, channel_multiplier=GN, allow_small_or_imprecise_dtypes=True).then_inc(consts, 1)
            nc.gpsimd.iota(iota_b[:, :], [[1, HN]], base=0, channel_multiplier=0, allow_small_or_imprecise_dtypes=True).then_inc(consts, 1)
            pool.wait_ge(first_set, 1)
            pool.wait_ge(win_built, 64)
            for k in range(2):
                for h in range(2):
                    nc.gpsimd.indirect_dma_start(out=win_i[k][0:G, h, :], out_offset=None, in_=win_tab[k][:, :],
                                                 in_offset=bass.IndirectOffsetOnAxis(ap=first_i[0:G, h:h + 1], axis=0)).then_inc(win_in, 16)
            pool.wait_ge(verdict_set, 1)
            regular = pool.value_load(regular_i[0:1, 0:1], min_val=0, max_val=1)
            with pool.If(regular == 1):
                fast_pool(pool)
            with pool.Else():
                slow_pool(pool)

        @block.vector
        def _(dve):
            n = [0]

            def step(ins):
                n[0] += 1
                ins.then_inc(chain, 1)
                dve.wait_ge(chain, n[0])

            dve.wait_ge(loaded, 16 * LOADS)
            dve.wait_ge(consts, 7)
            dve.wait_ge(consts, 13)
            for k, v in enumerate((src_i, dst_i)):
                nc.vector.tensor_copy(edge_f[k][:, :], v[:, :])
            step(nc.vector.memset(rt[:, :], 0.0))
            for j in range(5):
                last = nc.vector.tensor_scalar(below[:, j, :, :], tile_first[0:EP, :, :], edge_f[1][:, j * CS:j * CS + 1], None, ALU.is_gt)
            last.then_inc(below_set, 1)
            step(nc.vector.tensor_tensor(loop[:, :], edge_f[0][:, :], edge_f[1][:, :], ALU.is_equal))
            step(nc.vector.tensor_tensor_scan(rank[:, :], loop[:, :], loop[:, :], 0.0, ALU.add, ALU.max))
            nc.vector.tensor_copy(check[0:EP, 3:4], rank[:, ET - 1:ET]).then_inc(ranked, 1)
            dve.wait_ge(counted, 1)
            step(nc.vector.tensor_scalar(first_win[0:G, :], pD[1][0:G, 0:2], -1.0, 0.0, ALU.add, ALU.max))
            nc.vector.tensor_scalar(first_i[0:G, :], first_win[0:G, :], float(CL), None, ALU.min).then_inc(first_set, 1)
            dve.wait_ge(rank_off, 1)
            step(nc.vector.tensor_scalar(off1[0:EP, :], pD[0][0:EP, 0:1], -1.0, None, ALU.add))
            step(nc.vector.scalar_tensor_tensor(rank[:, :], rank[:, :], off1[0:EP, 0:1], edge_f[1][:, :], ALU.add, ALU.not_equal))
            step(nc.vector.tensor_tensor_reduce(out=edge_f[0][:, :], in0=rank[:, :], in1=loop[:, :], scale=1.0, scalar=0.0,
                                                op0=ALU.mult, op1=ALU.add, accum_out=check[0:EP, 0:1]))
            dve.wait_ge(win_in, 64)
            for k in range(2):
                last = nc.vector.tensor_copy(win_f[k][0:G, :, :], win_i[k][0:G, :, :])
            step(last)
            nc.vector.tensor_tensor(wa[0:G, :, :], win_f[0][0:G, :, :], win_f[1][0:G, :, :], ALU.not_equal)
            for h in range(2):
                last = nc.vector.tensor_scalar(wb[0:G, h, :], win_f[1][0:G, h, :], my_first[0:G, h:h + 1], None, ALU.subtract)
            step(last)
            step(nc.vector.scalar_tensor_tensor(wa[0:G, :, :], wb[0:G, :, :], 0.0, wa[0:G, :, :], ALU.is_ge, ALU.mult))
            step(nc.vector.scalar_tensor_tensor(wa[0:G, :, :], wb[0:G, :, :], float(HN), wa[0:G, :, :], ALU.is_lt, ALU.mult))
            step(nc.vector.tensor_reduce(check[0:G, 4:6], wa[0:G, :, :], mybir.AxisListType.X, ALU.add))
            step(nc.vector.scalar_tensor_tensor(wb[0:G, :, :], wb[0:G, :, :], float(KEY), win_f[0][0:G, :, :], ALU.mult, ALU.add))
            step(nc.vector.scalar_tensor_tensor(wb[0:G, :, :], wb[0:G, :, :], 1.0, wa[0:G, :, :], ALU.add, ALU.mult))
            step(nc.vector.tensor_scalar(wa[0:G, :, :], wb[0:G, :, :], -1.0, None, ALU.add))
            step(nc.vector.tensor_tensor(check[0:G, 2:3], check[0:G, 4:5], check[0:G, 5:6], ALU.add))
            step(nc.vector.tensor_scalar(off1[0:G, :], check[0:G, 4:5], float(SLOTS), None, ALU.is_gt))
            step(nc.vector.scalar_tensor_tensor(check[0:G, 1:2], check[0:G, 5:6], float(SLOTS), off1[0:G, :], ALU.is_gt, ALU.add))
            dve.sem_inc(checked, 1)
            dve.wait_ge(check_sum, 1)
            for k, want in enumerate((0, 0, E - N, N)):
                last = nc.vector.tensor_scalar(verdict[:, k:k + 1], pD[0][0:1, 8 + k:9 + k], float(want), None, ALU.is_equal)
            step(last)
            nc.vector.tensor_reduce(regular_i[:, 0:1], verdict[:, 0:4], mybir.AxisListType.X, ALU.min).then_inc(verdict_set, 1)
            dve.wait_ge(verdict_set, 1)
            regular = dve.value_load(regular_i[0:1, 0:1], min_val=0, max_val=1)
            with dve.If(regular == 1):
                fast_vector(dve, list(n))
            with dve.Else():
                slow_vector(dve, n, step)

        @block.scalar
        def _(act):
            for k, v in enumerate((src, dst)):
                act.dma_start(win_tab[k][0:CL, :], bass.AP(v.tensor, v.offset, [[CS, CL], [1, CW]])).then_inc(win_built, 16)
                act.dma_start(win_tab[k][CL:CL + 1, :], v[E - CW:E].rearrange("(o n) -> o n", o=1)).then_inc(win_built, 16)
            act.wait_ge(verdict_set, 1)
            regular = act.value_load(regular_i[0:1, 0:1], min_val=0, max_val=1)
            with act.If(regular == 1):
                fast_scalar(act)
            with act.Else():
                slow_scalar(act)

        @block.tensor
        def _(pe):
            pe.wait_ge(consts, 13)
            pe.wait_ge(below_set, 1)
            for h in range(2):
                for j in range(5):
                    last = nc.tensor.matmul(pD[1][0:G, h:h + 1], below[:, j, h, :], onesb[0:EP, 0:1], start=j == 0, stop=j == 4)
            last.then_inc(counted, 1)
            pe.wait_ge(ranked, 1)
            nc.tensor.matmul(pD[0][:, 0:1], upper[0:EP, :], check[0:EP, 3:4], start=True, stop=True).then_inc(rank_off, 1)
            pe.wait_ge(checked, 1)
            nc.tensor.matmul(pD[0][:, 8:12], ones[:, :], check[:, 0:4], start=True, stop=True).then_inc(check_sum, 1)
            pe.wait_ge(verdict_set, 1)
            regular = pe.value_load(regular_i[0:1, 0:1], min_val=0, max_val=1)
            with pe.If(regular == 1):
                fast_tensor(pe)
            with pe.Else():
                slow_tensor(pe)


_INS = ['x', 'src', 'dst', 'L0_gnn_W1', 'L0_gnn_b1', 'L0_gnn_W2', 'L0_gnn_b2', 'L1_gnn_We1', 'L1_gnn_be1', 'L1_gnn_We2',
        'L1_gnn_be2', 'L1_gnn_Wn1', 'L1_gnn_bn1', 'L1_gnn_Wn2', 'L1_gnn_bn2']


def kernel(**inputs):
    import numpy as _np
    import concourse.bacc as _bacc
    from concourse import mybir as _mybir
    from concourse.bass_utils import run_bass_kernel_spmd as _run

    nc = _bacc.Bacc("TRN2", target_bir_lowering=False, num_devices=1)
    arrays, args = {}, []
    for name in _INS:
        a = _np.ascontiguousarray(inputs[name])
        arrays[f"in_{name}_dram"] = a
        args.append(nc.dram_tensor(f"in_{name}_dram", a.shape, _mybir.dt.from_np(a.dtype), kind="ExternalInput").ap())
    args.append(nc.dram_tensor("out_0_dram", args[0].shape, F32, kind="ExternalOutput").ap())
    gnn(nc, *args)
    r = _run(nc, [arrays], core_ids=[0])
    return r.results[0]["out_0_dram"]
```

```python
from contextlib import ExitStack

import concourse.bass as bass
from concourse import mybir

F32 = mybir.dt.float32
BF16 = mybir.dt.bfloat16
I32 = mybir.dt.int32
F16 = mybir.dt.float16
ALU = mybir.AluOpType
ACT = mybir.ActivationFunctionType

P = 128
EPS = 1e-5


def gnn(nc, x, src, dst, W1, b1, W2, b2, We1, be1, We2, be2, Wn1, bn1, Wn2, bn2, out):
    N, D = x.shape
    E = src.shape[0]
    EP = 125
    ET = E // EP
    assert EP * ET == E and D == P
    B = 4
    GN = B * P
    G = -(-N // GN)
    NP = G * GN
    LASTP = (N - (G - 1) * GN) // B
    assert LASTP * B == N - (G - 1) * GN and G % 2 == 0
    TRASH = N

    with ExitStack() as ctx:
        def sb(name, shape, dt=F32):
            return ctx.enter_context(nc.sbuf_tensor(name, shape, dt))

        def ps(name, shape, dt=F32):
            return ctx.enter_context(nc.psum_tensor(name, shape, dt))

        def own(name):
            return ctx.enter_context(nc.semaphore(name))

        def table(name, cols=D):
            return nc.dram_tensor(name, [NP, cols], F32, kind="Internal").ap()

        agg_tab = [table("agg1_tab"), table("agg2_tab"), table("relu_tab")]
        hs_tab = table("hs_tab")
        x1_tab = table("x1_tab")
        norm_tab = nc.dram_tensor("norm_tab", [P * G * B, 1], F32, kind="Internal").ap()
        deg_tab = nc.dram_tensor("deg_tab", [G * B, P], F32, kind="Internal").ap()

        SLOTS = P

        early = sb("early", [P, G, 2, D])
        early_flat = early[:, :, :, :].rearrange("p g h d -> p (g h d)")
        taken = [0]

        def within(cols, dt=F32):
            taken[0] += cols
            part = early_flat[:, taken[0] - cols:taken[0]]
            return part if dt == F32 else part.bitcast(dt)

        src_i = sb("src_i", [EP, ET], I32)
        dst_i = sb("dst_i", [EP, ET], I32)
        nidx_i = within(ET, I32)[0:EP, :]
        code = [sb(f"code{k}", [EP, ET]) for k in range(4)]
        tmp_i = [within(ET, I32)[0:EP, :] for k in range(2)]
        dst_f = within(ET)[0:EP, :]
        iota_c = sb("iota_c", [P, G * B], F16)
        iota_p = sb("iota_p", [P, 1])
        trash = sb("trash", [P, 1])
        ident = sb("ident", [P, P])
        lower = sb("lower", [P, P])
        ones = sb("ones", [P, P])
        hot = [sb(f"hot{k}", [P, 2, P], BF16) for k in range(2)]
        hotc = [sb(f"hotc{k}", [P, 2, G * B], BF16) for k in range(2)]
        deg_out = sb("deg_out", [P, G * B])
        deg_in = sb("deg_in", [P, G * B])
        nsrc = sb("nsrc", [P, G * B])
        ndst = sb("ndst", [P, G * B])
        rt = sb("rt", [P, G * B])
        degT = sb("degT", [P, 4, P])
        zero = within(3584)

        w1 = sb("w1", [P, D]); w2 = sb("w2", [P, D])
        we1a = sb("we1a", [P, D]); we1b = sb("we1b", [P, D]); we2 = sb("we2", [P, D])
        wn1a = sb("wn1a", [P, D]); wn1b = sb("wn1b", [P, D]); wn2 = sb("wn2", [P, D])
        we2T = sb("we2T", [P, D])
        wf = sb("wf", [P, D])
        be2c = sb("be2c", [P, 1]); bn1c = sb("bn1c", [P, 1])
        vrow = sb("vrow", [1, D])
        b1b = sb("b1b", [P, D]); b2b = sb("b2b", [P, D]); be1b = sb("be1b", [P, D]); bn2b = sb("bn2b", [P, D])

        col = sb("col", [EP, 4], I32)
        rows = within(2 * D)[0:EP, :].rearrange("p (k d) -> p k d", k=2)
        nrow = sb("nrow", [EP, 1])
        dstB = within(EP)[0:EP, :]
        same = within(EP)[0:EP, :]
        junk = within(EP)[0:EP, :]
        cnt = sb("cnt", [EP, 4])
        scat_i = sb("scat_i", [EP, 1], I32)
        msg = within(D)[0:EP, :]
        comb = within(D)[0:EP, :]
        edT = within(2 * EP).rearrange("p (k e) -> p k e", k=2)

        ga = [sb(f"ga{k}", [P, B, D]) for k in range(2)]
        gx = [sb(f"gx{k}", [P, B, D]) for k in range(2)]
        gd = [within(GN)[0:1, :] for k in range(2)]
        aT = [sb(f"aT{k}", [P, GN]) for k in range(2)]
        xT = [sb(f"xT{k}", [P, GN]) for k in range(2)]
        mT = [sb(f"mT{k}", [P, GN]) for k in range(2)]
        y = [within(B * D).rearrange("p (i d) -> p i d", i=B) for k in range(2)]
        z = [sb(f"z{k}", [P, B, D]) for k in range(2)]
        go = [sb(f"go{k}", [P, B, D]) for k in range(2)]
        st = sb("st", [P, B, 6]); mv = sb("mv", [P, B, 2]); sd = sb("sd", [P, B]); rs = sb("rs", [P, B])
        eps = sb("eps", [P, 1])

        pA = [ps(f"pA{k}", [P, 512]) for k in range(2)]
        pB = [ps(f"pB{k}", [P, 512]) for k in range(2)]
        pC = [ps(f"pC{k}", [P, 512]) for k in range(2)]
        pD = [ps(f"pD{k}", [P, 512]) for k in range(2)]

        loaded = own("loaded"); consts = own("consts"); chain = own("chain")
        held = own("held"); held_dve = own("held_dve")
        ctx_sem = ExitStack()

        def sem(name):
            return ctx_sem.enter_context(nc.semaphore(name))

        zeroed = sem("zeroed"); zero_set = sem("zero_set")
        hot_ready = sem("hot_ready"); hist_done = sem("hist_done")
        deg_turn = sem("deg_turn"); deg_saved = sem("deg_saved"); norm_ready = sem("norm_ready"); tabs_saved = sem("tabs_saved")
        fuse_pe = sem("fuse_pe"); fuse_dve = sem("fuse_dve")
        col_ready = sem("col_ready"); rows_in = sem("rows_in"); rows2_in = sem("rows2_in"); nrow_in = sem("nrow_in")
        dst_spread = sem("dst_spread"); dst_turned = sem("dst_turned"); same_ready = sem("same_ready")
        scat_ready = sem("scat_ready"); msg_ready = sem("msg_ready"); summed = sem("summed"); comb_ready = sem("comb_ready")
        scattered = sem("scattered"); edge_turned = sem("edge_turned"); edge_copied = sem("edge_copied"); edge_mlp = sem("edge_mlp")
        edge_act = sem("edge_act")
        a_in = [[sem(f"a_in{s}{k}") for k in range(2)] for s in range(3)]
        x_in = [[sem(f"x_in{s}{k}") for k in range(2)] for s in range(3)]
        d_in = [sem(f"d_in{k}") for k in range(2)]
        turned = sem("turned"); copied = sem("copied"); mult = sem("mult"); hidden = sem("hidden"); mult2 = sem("mult2")
        group_out = [sem(f"group_out{k}") for k in range(2)]; var_ready = sem("var_ready"); sd_ready = sem("sd_ready")
        stored = [[sem(f"stored{s}{k}") for k in range(2)] for s in range(3)]
        ctx_sem.close()

        def tiles(eng, body):
            body(0)
            with eng.Fori(1, ET) as t:
                body(t)

        def wait(eng, semaphore, value):
            if not (isinstance(value, int) and value <= 0):
                eng.wait_ge(semaphore, value)

        def groups(eng, body):
            body(0, 0, 0)
            body(1, 1, 0)
            with eng.Fori(1, G // 2 - 1) as i:
                body(2 * i, 0, i)
                body(2 * i + 1, 1, i)
            body(G - 2, 0, G // 2 - 1)
            body(G - 1, 1, G // 2 - 1)

        def rows_of(t, g):
            return t.rearrange("(g p i) d -> g p i d", p=P, i=B)[bass.ds(g, 1)].rearrange("g p i d -> (g p) i d")



        SLOTS = P
        HN = GN // 2
        T = 2 * G
        WIN = HN + SLOTS
        CS = 100
        CW = WIN + CS
        CL = (E - CW) // CS + 1
        KEY = 1 << 16

        win_tab = [nc.dram_tensor(f"win_tab{k}", [CL + 1, CW], I32, kind="Internal").ap() for k in range(2)]
        vpart_tab = nc.dram_tensor("vpart_tab", [6, D], BF16, kind="Internal").ap()
        deg16_tab = nc.dram_tensor("deg16_tab", [G * B, P], BF16, kind="Internal").ap()

        regular_i = sb("regular_i", [1, 4], I32)
        upper = sb("upper", [P, P])
        edge_f, loop, rank = code[0:2], code[2], code[3]
        off1 = sb("off1", [P, 1])
        check = sb("check", [P, 8])
        verdict = sb("verdict", [1, 8])
        tile_first = sb("tile_first", [P, 2, G])
        below = sb("below", [EP, 5, 2, G], BF16)
        onesb = sb("onesb", [P, P], BF16)
        first_win = sb("first_win", [P, 2])
        first_i = sb("first_i", [P, 2], I32)
        my_first = sb("my_first", [P, 2])
        EARLY, LATER = 60, 80
        taken[0] = 0

        def halved(t):
            return t.rearrange("p (h w) -> p h w", h=2)
        win_i = [halved(within(2 * CW, I32)) for k in range(2)]
        win_f = [halved(within(2 * CW)) for k in range(2)]
        wa, wb = halved(within(2 * CW)), halved(within(2 * CW))
        taken[0] = 0
        keys = sb("keys", [P, 2, SLOTS])
        kT = sb("kT", [P, 2, G], I32)
        t0 = sb("t0", [P, 2, G], I32); t1 = sb("t1", [P, 2, G], I32); t2 = sb("t2", [P, 2, G], I32)
        sidx = sb("sidx", [P, 2, G], I32)
        didx = sb("didx", [P, 2, G], I32)
        nidx = sb("nidx", [P, 2, G], I32)
        dcode = sb("dcode", [P, 2, G])
        srow = sb("srow", [P, 2, G]); scol = sb("scol", [P, 2, G])
        dq = sb("dq", [P, 2, G], BF16)
        di = sb("di", [P, 2, G], BF16)
        iota_b = sb("iota_b", [P, HN], BF16)
        late = sb("late", [P, 7, GN])
        hp = late[:, :, :].rearrange("p k n -> p (k n)")[:, 0:G * 32].bitcast(BF16).rearrange("p (g q) -> p g q", g=G)

        def rows4(k):
            return late[:, k, :].rearrange("p (i d) -> p i d", i=B)
        hi = sb("hi", [P, G, B], BF16)
        degT16 = sb("degT16", [P, 4, P], BF16)
        wes = sb("wes", [P, D])
        be1c = sb("be1c", [P, 1])
        be1r = sb("be1r", [1, D])
        vparts = sb("vparts", [1, 6, D], BF16)
        vres = sb("vres", [1, 2, D])
        vp3 = sb("vp3", [3, 2, D], BF16)
        fcol = [sb(f"fcol{r}", [P, 4], I32) for r in range(4)]
        fx = gx + [rows4(0), rows4(1)]
        fx2 = [within(B * D).rearrange("p (i d) -> p i d", i=B) for r in range(4)]
        fr = ga + [rows4(2), rows4(3)]
        fn = [sb(f"fn{r}", [P, 2]) for r in range(4)]
        fd = [sb(f"fd{r}", [3, GN], BF16) for r in range(4)]
        fhot = [sb("fhot0", [P, 2, HN]), late[:, 6, :].rearrange("p (h n) -> p h n", h=2)]
        fy = [within(B * D).rearrange("p (i d) -> p i d", i=B) for r in range(4)]
        fe = [within(GN) for r in range(2)]
        fs = [within(GN) for r in range(2)]
        fm = [sb(f"fm{r}", [P, 2, D]) for r in range(2)]
        mparts = [[halved(within(D, BF16)) for part in range(3)] for r in range(2)]
        hot16 = [halved(within(HN, BF16)) for r in range(2)]
        fo = go + [rows4(4), rows4(5)]
        fst = [sb(f"fst{r}", [P, B, 6]) for r in range(4)]
        fmv = [sb(f"fmv{r}", [P, B, 2]) for r in range(4)]
        fsd = [sb(f"fsd{r}", [P, B]) for r in range(4)]
        frs = [sb(f"frs{r}", [P, B]) for r in range(4)]
        fnm = [sb(f"fnm{r}", [P, B]) for r in range(4)]

        ranked = own("ranked"); rank_off = own("rank_off"); win_built = own("win_built"); below_set = own("below_set")
        counted = own("counted"); first_set = own("first_set"); win_in = own("win_in"); checked = own("checked"); check_sum = own("check_sum")
        verdict_set = own("verdict_set")
        keys_set = own("keys_set"); keys_turned = own("keys_turned"); slots_set = own("slots_set")
        f_hot = own("f_hot"); f_hist = own("f_hist"); f_hp = own("f_hp"); f_in = own("f_in"); f_recip = own("f_recip"); f_norm = own("f_norm")
        f_degt = own("f_degt"); f_deg16 = own("f_deg16"); f_tabs = own("f_tabs"); f_fuse_pe = own("f_fuse_pe"); f_fuse = own("f_fuse"); f_parts = own("f_parts"); f_parts_in = own("f_parts_in")
        f_clean = own("f_clean"); norm_saved = own("norm_saved"); early_in = own("early_in"); late_in = [own(f"late_in{k}") for k in range(2)]

        class Phase:
            def __init__(self, s):
                def four(name):
                    return [own(f"{name}_{s}_{r}") for r in range(4)]
                self.x_in = four("rows_of_group")
                self.x2_in = four("x_of_group") if s == 1 else None
                self.d_in = four("degrees_of_group") if s == 2 else None
                self.gathered = four("gathered")
                self.stored = four("stored")
                self.col_set = own(f"col_set_{s}")
                self.hot_set = own(f"hot_set_{s}")
                self.summed = own(f"summed_{s}")
                self.evacuated = own(f"evacuated_{s}")
                self.mixed = own(f"mixed_{s}")
                self.scaled_msg = own(f"scaled_msg_{s}") if s == 0 else None
                self.scaled = own(f"scaled_{s}")
                if s == 2:
                    self.msgs = own(f"msgs_{s}")
                    self.rest = own(f"rest_{s}")
                    self.parted = own(f"parted_{s}")
                self.rsum = own(f"rsum_{s}")
                self.radd = own(f"radd_{s}")
                self.hid = own(f"hid_{s}")
                self.hidact = own(f"hidact_{s}")
                self.outp = own(f"outp_{s}")
                self.posted = own(f"posted_{s}")
                self.rooted = own(f"rooted_{s}")
                self.recip = own(f"recip_{s}")
                self.inverted = own(f"inverted_{s}")
                self.result = own(f"result_{s}")
        phases = [Phase(s) for s in range(3)]

        LOADS = 2 + 8 + 2 + 4 + 2
        def v3(t):
            return t.rearrange("p (i d) -> p i d", i=B)

        class At:

            def __init__(self, g, r, u):
                self.g, self.r, self.u = g, r, u
                self.b = r % 2

        def pipeline(eng, body, lead, lag, peel=1, breaks=()):
            def fixed(j):
                def at(d):
                    g = j + d
                    return At(g, g % 4, g // 4) if 0 <= g < G else None
                return at

            def turning(i, jm):
                def at(d):
                    k = jm + d
                    return At(4 * i + k, k % 4, i + k // 4)
                return at
            for j in range(-lead, 4 * peel):
                body(fixed(j))
            turns = (G - lead) // 4
            start = peel
            for turn, action in (*breaks, (turns, None)):
                if start < turn:
                    with eng.Fori(start, turn) as i:
                        for jm in range(4):
                            body(turning(i, jm))
                start = turn
                if action:
                    action()
            for j in range(4 * turns, G + lag):
                body(fixed(j))

        def after(eng, semaphore, at, back=0):
            wait(eng, semaphore, at.g + (1 - back))

        def landed(eng, semaphore, at, dmas=1, back=0):
            wait(eng, semaphore[at.r], at.u * (16 * dmas) + 16 * dmas * (1 - back))

        def tables_complete(eng, s):
            for r in range(4):
                eng.wait_ge(phases[s].stored[r], 16 * len(range(r, G, 4)))
        def slow_sync(sp):
            sp.wait_ge(zero_set, 1)
            nz = 0
            for t in agg_tab:
                tz = t.rearrange("(c p q) d -> c p (q d)", p=P, q=3584 // D)
                for c in range(tz.shape[0]):
                    sp.dma_start(tz[c], zero[:, :]).then_inc(zeroed, 16)
                    nz += 1
            assert nz == 3 * NP * D // (P * 3584)
            sp.wait_ge(norm_ready, 2)
            sp.dma_start(norm_tab.rearrange("(p c) o -> p (c o)", p=P), nsrc[:, :]).then_inc(tabs_saved, 16)
            sp.wait_ge(deg_saved, 4)
            for c in range(4):
                m = min(P, G * B - c * P)
                sp.dma_start(deg_tab[c * P:c * P + m, :], degT[0:m, c, :]).then_inc(tabs_saved, 16)
            for s in range(3):
                sp.wait_ge(scattered, 16 * ET * (s + 1))
                if s == 2:
                    sp.wait_ge(tabs_saved, 16 * 5)

                def load(g, b, u, s=s):
                    wait(sp, group_out[b], s * (G // 2) + u)
                    sp.dma_start(ga[b][:, :, :], rows_of(agg_tab[s], g)).then_inc(a_in[s][b], 16)
                    if s == 1:
                        if isinstance(g, int) and g == G - 1:
                            sp.dma_start(gx[b][0:LASTP, :, :], x[(G - 1) * GN:N, :].rearrange("(p i) d -> p i d", i=B)).then_inc(x_in[s][b], 16)
                        else:
                            sp.dma_start(gx[b][:, :, :], x[bass.ds(g * GN, GN), :].rearrange("(p i) d -> p i d", i=B)).then_inc(x_in[s][b], 16)
                    if s == 2:
                        sp.dma_start(gx[b][:, :, :], rows_of(x1_tab, g)).then_inc(x_in[s][b], 16)
                        sp.dma_start(gd[b][:, :], deg_tab.rearrange("(g i) p -> g (i p)", i=B)[bass.ds(g, 1), :]).then_inc(d_in[b], 16)
                groups(sp, load)

        def slow_pool(pool):
            nc.gpsimd.memset(zero[:, :], 0.0).then_inc(zero_set, 1)
            pool.wait_ge(zeroed, 16 * 42)
            pool.wait_ge(tabs_saved, 16 * 5)
            feat = [x, hs_tab, x1_tab]
            for s in range(3):
                if s:
                    for b in range(2):
                        pool.wait_ge(stored[s - 1][b], 16 * (G // 2))
                def edges(t, s=s):
                    nc.gpsimd.tensor_copy(col[:, 0:1], src_i[:, bass.ds(t, 1)])
                    nc.gpsimd.tensor_copy(col[:, 1:2], dst_i[:, bass.ds(t, 1)])
                    nc.gpsimd.tensor_copy(col[:, 2:3], nidx_i[:, bass.ds(t, 1)]).then_inc(col_ready, 1)
                    pool.wait_ge(col_ready, t + 1 + s * ET)
                    pool.sem_inc(held, 1)
                    nc.gpsimd.indirect_dma_start(out=rows[:, 0, :], out_offset=None, in_=feat[s][:, :],
                                                 in_offset=bass.IndirectOffsetOnAxis(ap=col[:, 0:1], axis=0)).then_inc(rows_in, 16)
                    if s == 0:
                        nc.gpsimd.indirect_dma_start(out=nrow[:, :], out_offset=None, in_=norm_tab[:, :],
                                                     in_offset=bass.IndirectOffsetOnAxis(ap=col[:, 2:3], axis=0)).then_inc(nrow_in, 16)
                    if s == 2:
                        nc.gpsimd.indirect_dma_start(out=rows[:, 1, :], out_offset=None, in_=feat[s][:, :],
                                                     in_offset=bass.IndirectOffsetOnAxis(ap=col[:, 1:2], axis=0)).then_inc(rows2_in, 16)
                    pool.wait_ge(scat_ready, t + 1 + s * ET)
                    pool.wait_ge(comb_ready, t + 1 + s * ET)
                    pool.sem_inc(held, 1)
                    nc.gpsimd.indirect_dma_start(out=agg_tab[s][:, :], out_offset=bass.IndirectOffsetOnAxis(ap=scat_i[:, 0:1], axis=0),
                                                 in_=comb[:, :], in_offset=None, compute_op=ALU.add).then_inc(scattered, 16)
                    pool.wait_ge(scattered, 16 * t + (16 + s * ET * 16))
                tiles(pool, edges)

        def slow_vector(dve, n, step):
            for k, v in enumerate((src_i, dst_i)):
                step(nc.vector.tensor_scalar(tmp_i[0][:, :], v[:, :], 2, 127, ALU.logical_shift_right, ALU.bitwise_and))
                step(nc.vector.tensor_copy(code[2 * k][:, :], tmp_i[0][:, :]))
                step(nc.vector.tensor_scalar(tmp_i[0][:, :], v[:, :], 9, 2, ALU.logical_shift_right, ALU.logical_shift_left))
                step(nc.vector.tensor_scalar(tmp_i[1][:, :], v[:, :], 3, None, ALU.bitwise_and))
                step(nc.vector.tensor_tensor(code[2 * k + 1][:, :], tmp_i[0][:, :], tmp_i[1][:, :], ALU.add))
            step(nc.vector.scalar_tensor_tensor(nidx_i[:, :], code[0][:, :], float(G * B), code[1][:, :], ALU.mult, ALU.add))
            step(nc.vector.tensor_copy(dst_f[:, :], dst_i[:, :]))
            def hots(b, t, u):
                wait(dve, hist_done, u)
                for k in range(2):
                    nc.vector.tensor_scalar(hot[b][0:EP, k, :], iota_c[0:EP, 0:P], code[2 * k][:, bass.ds(t, 1)], None, ALU.is_equal)
                    last = nc.vector.tensor_scalar(hotc[b][0:EP, k, :], iota_c[0:EP, :], code[2 * k + 1][:, bass.ds(t, 1)], None, ALU.is_equal)
                last.then_inc(hot_ready, 1)
            hots(0, 0, 0)
            hots(1, 1, 0)
            with dve.Fori(1, ET // 2) as i:
                hots(0, 2 * i, i)
                hots(1, 2 * i + 1, i)
            dve.wait_ge(hist_done, ET // 2)
            step(nc.vector.tensor_copy(deg_out[:, :], pA[0][:, 0:G * B]))
            step(nc.vector.tensor_copy(deg_in[:, :], pA[1][:, 0:G * B]))
            for k, (d, r) in enumerate(((deg_out, nsrc), (deg_in, ndst))):
                step(nc.vector.tensor_scalar(rt[:, :], d[:, :], 1.0, None, ALU.max))
                inv = nc.vector.reciprocal(r[:, :], rt[:, :])
                if k == 0:
                    step(inv)
            inv.then_inc(fuse_dve, 1)
            dve.wait_ge(deg_turn, 1)
            for c in range(4):
                m = min(P, G * B - c * P)
                nc.vector.tensor_copy(degT[0:m, c, :], pB[0][0:m, c * P:(c + 1) * P]).then_inc(deg_saved, 1)
            dve.wait_ge(fuse_pe, 1)
            nc.vector.tensor_copy(we2T[:, :], pB[1][:, 0:D]).then_inc(fuse_dve, 1)
            dve.wait_ge(fuse_pe, 2)
            nc.vector.tensor_copy(wf[:, :], pB[1][:, 128:128 + D])
            nc.vector.tensor_copy(vrow[:, :], pB[1][0:1, 256:256 + D]).then_inc(fuse_dve, 1)
            dve.wait_ge(norm_ready, 2)
            for s in range(3):
                def edges(t, s=s, n0=n[0]):
                    wait(dve, comb_ready, t + s * ET)
                    wait(dve, scattered, 16 * t + s * ET * 16)
                    nc.vector.tensor_copy(dstB[:, :], dst_f[:, bass.ds(t, 1)].to_broadcast([EP, EP]))
                    nc.vector.tensor_copy(cnt[:, 2:3], dst_f[:, bass.ds(t, 1)]).then_inc(dst_spread, 1)
                    dve.wait_ge(dst_turned, t + 1 + s * ET)
                    dve.wait_ge(dst_spread, t + 1 + s * ET)
                    nc.vector.tensor_scalar(same[:, :], pA[0][0:EP, 0:EP], cnt[:, 2:3], None, ALU.is_equal).then_inc(same_ready, 1)
                    dve.wait_ge(same_ready, t + 1 + s * ET)
                    nc.vector.tensor_tensor_reduce(out=junk[:, :], in0=same[:, :], in1=lower[0:EP, 0:EP], scale=1.0, scalar=0.0,
                                                   op0=ALU.mult, op1=ALU.add, accum_out=cnt[:, 0:1]).then_inc(chain, 1)
                    dve.wait_ge(chain, t * 4 + (n0 + 1))
                    nc.vector.tensor_scalar(cnt[:, 1:2], cnt[:, 0:1], 0.5, None, ALU.is_lt).then_inc(chain, 1)
                    nc.vector.tensor_tensor(cnt[:, 3:4], cnt[:, 2:3], trash[0:EP, :], ALU.subtract).then_inc(chain, 1)
                    dve.wait_ge(chain, t * 4 + (n0 + 3))
                    nc.vector.tensor_tensor(cnt[:, 0:1], cnt[:, 1:2], cnt[:, 3:4], ALU.mult).then_inc(chain, 1)
                    dve.wait_ge(chain, t * 4 + (n0 + 4))
                    nc.vector.tensor_tensor(scat_i[:, :], cnt[:, 0:1], trash[0:EP, :], ALU.add).then_inc(scat_ready, 1)
                    if s == 0:
                        dve.wait_ge(rows_in, 16 * t + 16)
                        dve.wait_ge(nrow_in, 16 * t + 16)
                        nc.vector.tensor_scalar(msg[:, :], rows[:, 0, :], nrow[:, 0:1], None, ALU.mult).then_inc(msg_ready, 1)
                    if s == 2:
                        dve.wait_ge(edge_mlp, t + 1)
                        nc.vector.tensor_tensor(msg[:, :], pC[0][0:EP, 0:D], be1b[0:EP, :], ALU.add).then_inc(edge_act, 1)
                        dve.wait_ge(edge_act, t + 1)
                        nc.vector.tensor_scalar(msg[:, :], msg[:, :], 0.0, None, ALU.max).then_inc(msg_ready, 1)
                    dve.wait_ge(summed, t + 1 + s * ET)
                    nc.vector.tensor_copy(comb[:, :], pD[0][0:EP, 0:D]).then_inc(comb_ready, 1)
                tiles(dve, edges)
                n[0] += 4 * ET

                def bc(v, g):
                    return v[:, bass.ds(g * B, B)].rearrange("p (i o) -> p i o", o=1).to_broadcast([P, B, D])

                def bd(v):
                    return v[:, :].rearrange("p (o d) -> p o d", o=1).to_broadcast([P, B, D])

                per = {0: 3, 1: 5, 2: 4}[s]
                base = n[0]

                def post(g, b, u, s=s, per=per, base=base):
                    c = [0]

                    def link(ins):
                        c[0] += 1
                        ins.then_inc(chain, 1)
                        dve.wait_ge(chain, g * per + (base + c[0]))

                    def v3(t):
                        return t.rearrange("p (i d) -> p i d", i=B)

                    done = s * G + g
                    if s < 2:
                        dve.wait_ge(mult, done + 1)
                        link(nc.vector.tensor_tensor(y[b][:, :, :], v3(pB[b][:, :]), bc(ndst, g), ALU.mult))
                        link(nc.vector.tensor_tensor(z[b][:, :, :], y[b][:, :, :], bd(b1b if s == 0 else b2b), ALU.add))
                    if s == 0:
                        wait(dve, stored[s][b], 16 * u)
                        link(nc.vector.tensor_scalar(y[b][:, :, :], z[b][:, :, :], 0.0, None, ALU.max))
                        last = nc.vector.tensor_tensor(go[b][:, :, :], y[b][:, :, :], bc(nsrc, g), ALU.mult)
                    else:
                        dve.wait_ge(x_in[s][b], 16 * u + 16)
                        if s == 1:
                            link(nc.vector.scalar_tensor_tensor(y[b][:, :, :], z[b][:, :, :], 0.0, gx[b][:, :, :], ALU.max, ALU.add))
                        else:
                            dve.wait_ge(mult2, g + 1)
                            link(nc.vector.tensor_tensor(z[b][:, :, :], v3(pD[b][:, :]), bd(bn2b), ALU.add))
                            link(nc.vector.scalar_tensor_tensor(y[b][:, :, :], gx[b][:, :, :], 2.0, z[b][:, :, :], ALU.mult, ALU.add))
                        for i in range(B):
                            last = nc.vector.bn_stats(st[:, i, :], y[b][:, i, :])
                        link(last)
                        dve.sem_inc(held_dve, 1)
                        for i in range(B):
                            last = nc.vector.bn_aggr(mv[:, i, :], st[:, i, :])
                        last.then_inc(var_ready, 1)
                        dve.wait_ge(sd_ready, (s - 1) * G + g + 1)
                        link(nc.vector.reciprocal(rs[:, :], sd[:, :]))
                        wait(dve, stored[s][b], 16 * u)
                        for i in range(B):
                            last = nc.vector.tensor_scalar(go[b][:, i, :], y[b][:, i, :], mv[:, i, 0:1], rs[:, i:i + 1], ALU.subtract, ALU.mult)
                    assert c[0] == per
                    last.then_inc(group_out[b], 1)
                groups(dve, post)
                n[0] += per * G

        def slow_scalar(act):
            act.wait_ge(fuse_dve, 1)
            nc.scalar.activation(nsrc[:, :], nsrc[:, :], ACT.Sqrt).then_inc(norm_ready, 1)
            nc.scalar.activation(ndst[:, :], ndst[:, :], ACT.Sqrt).then_inc(norm_ready, 1)
            for s in range(3):
                if s:
                    act.wait_ge(loaded, 16 * LOADS)
                if s == 2:
                    def edges(t):
                        act.wait_ge(edge_turned, t + 1)
                        nc.scalar.copy(edT[:, :, :], pB[0][:, 0:2 * EP].rearrange("p (k e) -> p k e", k=2)).then_inc(edge_copied, 1)
                    tiles(act, edges)

                def pre(g, b, u, s=s):
                    act.wait_ge(turned, s * G + g + 1)
                    nc.scalar.copy(aT[b][:, :], pA[b][:, :]).then_inc(copied, 1)
                    if s == 2:
                        nc.scalar.copy(xT[b][:, :], pC[b][:, :]).then_inc(copied, 1)
                        act.wait_ge(mult, s * G + g + 1)
                        nc.scalar.activation(mT[b][:, :], pB[b][:, :], ACT.Relu, bias=bn1c[:, 0:1]).then_inc(hidden, 1)
                    if s:
                        act.wait_ge(var_ready, (s - 1) * G + g + 1)
                        nc.scalar.activation(sd[:, :], mv[:, :, 1], ACT.Sqrt, bias=eps[:, 0:1]).then_inc(sd_ready, 1)
                    act.wait_ge(group_out[b], s * (G // 2) + u + 1)
                    if s < 2:
                        act.dma_start(rows_of(hs_tab if s == 0 else x1_tab, g), go[b][:, :, :]).then_inc(stored[s][b], 16)
                    elif isinstance(g, int) and g == G - 1:
                        act.dma_start(out[(G - 1) * GN:N, :].rearrange("(p i) d -> p i d", i=B), go[b][0:LASTP, :, :]).then_inc(stored[s][b], 16)
                    else:
                        act.dma_start(out[bass.ds(g * GN, GN), :].rearrange("(p i) d -> p i d", i=B), go[b][:, :, :]).then_inc(stored[s][b], 16)
                groups(act, pre)
            for b in range(2):
                act.wait_ge(stored[2][b], 16 * (G // 2))

        def slow_tensor(pe):
            def hist(b, t, i, start=False, stop=False):
                pe.wait_ge(hot_ready, t + 1)
                for k in range(2):
                    last = nc.tensor.matmul(pA[k][:, 0:G * B], hot[b][0:EP, k, :], hotc[b][0:EP, k, :], start=start, stop=stop)
                return last
            hist(0, 0, 0, start=True)
            hist(1, 1, 0).then_inc(hist_done, 1)
            with pe.Fori(1, ET // 2 - 1) as i:
                hist(0, 2 * i, i)
                hist(1, 2 * i + 1, i).then_inc(hist_done, 1)
            hist(0, ET - 2, 0)
            hist(1, ET - 1, 0, stop=True).then_inc(hist_done, 1)
            pe.wait_ge(fuse_dve, 1)
            for c in range(4):
                m = min(P, G * B - c * P)
                last = nc.tensor.transpose(pB[0][0:m, c * P:(c + 1) * P], deg_in[:, c * P:c * P + m], ident[:, :])
            last.then_inc(deg_turn, 1)
            nc.tensor.transpose(pB[1][:, 0:D], we2[:, :], ident[:, :]).then_inc(fuse_pe, 1)
            pe.wait_ge(fuse_dve, 2)
            nc.tensor.matmul(pB[1][:, 128:128 + D], we2T[:, :], wn1b[:, :], start=True, stop=True)
            nc.tensor.matmul(pB[1][0:1, 256:256 + D], be2c[:, :], wn1b[:, :], start=True, stop=True).then_inc(fuse_pe, 1)
            pe.wait_ge(fuse_dve, 3)
            pe.wait_ge(deg_saved, 4)
            for s in range(3):
                def edges(t, s=s):
                    pe.wait_ge(dst_spread, t + 1 + s * ET)
                    nc.tensor.transpose(pA[0][0:EP, 0:EP], dstB[:, :], ident[0:EP, 0:EP]).then_inc(dst_turned, 1)
                    if s == 2:
                        pe.wait_ge(rows_in, 16 * t + (16 + s * ET * 16))
                        pe.wait_ge(rows2_in, 16 * t + 16)
                        for k in range(2):
                            last = nc.tensor.transpose(pB[0][:, k * EP:(k + 1) * EP], rows[:, k, :], ident[0:EP, 0:EP])
                        last.then_inc(edge_turned, 1)
                        pe.wait_ge(edge_copied, t + 1)
                        nc.tensor.matmul(pC[0][0:EP, 0:D], edT[:, 0, :], we1a[:, :], start=True, stop=False)
                        nc.tensor.matmul(pC[0][0:EP, 0:D], edT[:, 1, :], we1b[:, :], start=False, stop=True).then_inc(edge_mlp, 1)
                    pe.wait_ge(same_ready, t + 1 + s * ET)
                    if s == 1:
                        pe.wait_ge(rows_in, 16 * t + (16 + s * ET * 16))
                        m = rows[:, 0, :]
                    else:
                        pe.wait_ge(msg_ready, t + 1 + (ET if s == 2 else 0))
                        m = msg[:, :]
                    nc.tensor.matmul(pD[0][0:EP, 0:D], same[:, :], m, start=True, stop=True).then_inc(summed, 1)
                tiles(pe, edges)

                def mm(g, b, u, s=s):
                    wait(pe, group_out[b], s * (G // 2) + u)
                    pe.wait_ge(a_in[s][b], 16 * u + 16)
                    if s == 2:
                        pe.wait_ge(x_in[s][b], 16 * u + 16)
                    for i in range(B):
                        last = nc.tensor.transpose(pA[b][:, i * P:(i + 1) * P], ga[b][:, i, :], ident[:, :])
                        if s == 2:
                            last = nc.tensor.transpose(pC[b][:, i * P:(i + 1) * P], gx[b][:, i, :], ident[:, :])
                    last.then_inc(turned, 1)
                    if s < 2:
                        pe.wait_ge(copied, s * G + g + 1)
                        for i in range(B):
                            last = nc.tensor.matmul(pB[b][:, i * P:(i + 1) * P], aT[b][:, i * P:(i + 1) * P],
                                                    (w1 if s == 0 else w2)[:, :], start=True, stop=True)
                        last.then_inc(mult, 1)
                    else:
                        pe.wait_ge(copied, 2 * g + (2 * G + 2))
                        nc.tensor.matmul(pB[b][:, :], wn1a[:, :], xT[b][:, :], start=True, stop=False)
                        nc.tensor.matmul(pB[b][:, :], wf[:, :], aT[b][:, :], start=False, stop=False)
                        pe.wait_ge(d_in[b], 16 * u + 16)
                        nc.tensor.matmul(pB[b][:, :], vrow[:, :], gd[b][:, :], start=False, stop=True).then_inc(mult, 1)
                        pe.wait_ge(hidden, g + 1)
                        for i in range(B):
                            last = nc.tensor.matmul(pD[b][:, i * P:(i + 1) * P], mT[b][:, i * P:(i + 1) * P], wn2[:, :], start=True, stop=True)
                        last.then_inc(mult2, 1)
                groups(pe, mm)

        def fast_sync(sp):
            sp.wait_ge(f_norm, 1)
            sp.dma_start(norm_tab.rearrange("(p c) o -> p (c o)", p=P), nsrc[:, :]).then_inc(norm_saved, 16)
            for s in range(3):
                ph = phases[s]
                if s:
                    tables_complete(sp, s - 1)
                if s == 1:
                    sp.wait_ge(f_deg16, 4)
                    for c in range(4):
                        m = min(P, G * B - c * P)
                        sp.dma_start(deg16_tab[c * P:c * P + m, :], degT16[0:m, c, :]).then_inc(f_tabs, 16)
                    sp.wait_ge(f_parts, 1)
                    sp.dma_start(vpart_tab.rearrange("(o k) d -> o k d", o=1), vparts[:, :, :]).then_inc(f_parts_in, 16)
                if s == 2:
                    sp.wait_ge(f_parts_in, 16)
                    sp.dma_start(vp3[:, :, :], vpart_tab.rearrange("(k v) d -> k v d", v=2)).then_inc(f_parts_in, 16)
                    sp.wait_ge(f_tabs, 16 * 4)

                lag = 6

                def load(g, rows, table, arrived):
                    if table is x and isinstance(g.g, int) and g.g == G - 1:
                        sp.dma_start(rows[g.r][0:LASTP, :, :], x[(G - 1) * GN:N, :].rearrange("(p i) d -> p i d", i=B)).then_inc(arrived[g.r], 16)
                    else:
                        sp.dma_start(rows[g.r][:, :, :], table[bass.ds(g.g * GN, GN), :].rearrange("(p i) d -> p i d", i=B)).then_inc(arrived[g.r], 16)

                def body(at, s=s, ph=ph, lag=lag, load=load):
                    g = at(0)
                    if g:
                        if s == 0:
                            after(sp, ph.hot_set, g, 4)
                        elif s == 1:
                            after(sp, ph.summed, g, 4)
                        else:
                            after(sp, ph.posted, g, 4)
                            after(sp, ph.hid, g, 4)
                        sp.sem_inc(held, 1)
                        load(g, fx, (x, hs_tab, x1_tab)[s], ph.x_in)
                        if s == 2:
                            sp.dma_start(fd[g.r][:, :], deg16_tab.rearrange("(g i) p -> g (i p)", i=B)[bass.ds(g.g, 1), :].to_broadcast([3, GN])).then_inc(ph.d_in[g.r], 16)
                    if s == 1 and at(-2):
                        after(sp, ph.posted, at(-2), 4)
                        sp.sem_inc(held, 1)
                        load(at(-2), fx2, x, ph.x2_in)
                    g = at(-lag)
                    if g:
                        after(sp, ph.result, g)
                        sp.sem_inc(held, 1)
                        if s < 2:
                            sp.dma_start((hs_tab, x1_tab)[s][bass.ds(g.g * GN, GN), :].rearrange("(p i) d -> p i d", i=B), fo[g.r][:, :, :]).then_inc(ph.stored[g.r], 16)
                        elif isinstance(g.g, int) and g.g == G - 1:
                            sp.dma_start(out[(G - 1) * GN:N, :].rearrange("(p i) d -> p i d", i=B), fo[g.r][0:LASTP, :, :]).then_inc(ph.stored[g.r], 16)
                        else:
                            sp.dma_start(out[bass.ds(g.g * GN, GN), :].rearrange("(p i) d -> p i d", i=B), fo[g.r][:, :, :]).then_inc(ph.stored[g.r], 16)
                pipeline(sp, body, 0, lag, 2)
            tables_complete(sp, 2)

        def fast_pool(pool):
            for r in range(4):
                nc.gpsimd.memset(fr[r][:, :, :], 0.0).then_inc(f_clean, 1)
                nc.gpsimd.memset(fn[r][:, :], 0.0).then_inc(f_clean, 1)
            nc.gpsimd.memset(early_flat[:, 12 * CW:], 0.0).then_inc(f_clean, 1)
            pool.wait_ge(f_clean, 9)
            pool.wait_ge(slots_set, 1)
            def x_of_sources(groups, arrived):
                for g in groups:
                    for h in range(2):
                        nc.gpsimd.indirect_dma_start(out=early[:, g, h, :], out_offset=None, in_=x[:, :],
                                                     in_offset=bass.IndirectOffsetOnAxis(ap=sidx[:, h, g:g + 1], axis=0),
                                                     bounds_check=N - 1, oob_is_err=False).then_inc(arrived, 16)
            x_of_sources(range(EARLY), early_in)
            pool.wait_ge(norm_saved, 16)
            for s in range(3):
                ph = phases[s]
                if s:
                    tables_complete(pool, s - 1)
                n_rows = 4 if s == 2 else 2

                def body(at, s=s, ph=ph, n_rows=n_rows):
                    g = at(1)
                    if g:
                        landed(pool, ph.gathered, g, n_rows, 1)
                        last = nc.gpsimd.tensor_copy(fcol[g.r][:, 0:2], (sidx if s else nidx)[:, :, bass.ds(g.g, 1)].rearrange("p h o -> p (h o)"))
                        if s == 2:
                            last = nc.gpsimd.tensor_copy(fcol[g.r][:, 2:4], didx[:, :, bass.ds(g.g, 1)].rearrange("p h o -> p (h o)"))
                        last.then_inc(ph.col_set, 1)
                    g = at(0)
                    if g:
                        after(pool, ph.col_set, g)
                        after(pool, ph.summed, g, 4)
                        pool.sem_inc(held, 1)
                        for k in range(n_rows):
                            if s == 0:
                                dest, tab, bound = fn[g.r][:, k:k + 1], norm_tab, P * G * B - 1
                            else:
                                dest, tab, bound = fr[g.r][:, k, :], (None, hs_tab, x1_tab)[s], N - 1
                            nc.gpsimd.indirect_dma_start(out=dest, out_offset=None, in_=tab[:, :],
                                                         in_offset=bass.IndirectOffsetOnAxis(ap=fcol[g.r][:, k:k + 1], axis=0),
                                                         bounds_check=bound, oob_is_err=False).then_inc(ph.gathered[g.r], 16)
                def late_rows(k):
                    first = EARLY + 2 * (k - 1)
                    x_of_sources(range(first, first + 2), late_in[0 if first < LATER else 1])
                pipeline(pool, body, 1, 0, 1, [(k, lambda k=k: late_rows(k)) for k in range(1, 1 + (G - EARLY) // 2)] if s == 0 else ())

        def fast_vector(dve, n):
            def step(ins):
                n[0] += 1
                ins.then_inc(chain, 1)
                dve.wait_ge(chain, n[0])

            for k in range(SLOTS // 8):
                for h in range(2):
                    last = nc.vector.max(keys[0:G, h, 8 * k:8 * k + 8], wa[0:G, h, :])
                step(last)
                if k < SLOTS // 8 - 1:
                    for h in range(2):
                        last = nc.vector.match_replace(wa[0:G, h, :], keys[0:G, h, 8 * k:8 * k + 8], wa[0:G, h, :], -1.0)
                    step(last)
            dve.sem_inc(keys_set, 1)
            dve.wait_ge(keys_turned, 1)
            step(nc.vector.tensor_copy(kT[:, :, :], pA[0][:, 0:T].rearrange("p (h g) -> p h g", h=2)))

            def bits(dest, of, a, b, opa, opb=None):
                step(nc.vector.tensor_scalar(dest[:, :, :], of[:, :, :], a, b, opa, opb) if opb is not None
                     else nc.vector.tensor_scalar(dest[:, :, :], of[:, :, :], a, None, opa))
            SHR, SHL, AND = ALU.logical_shift_right, ALU.logical_shift_left, ALU.bitwise_and
            bits(sidx, kT, KEY - 1, None, AND)
            bits(t0, kT, 16, None, SHR)
            step(nc.vector.tensor_tensor(didx[:, :, :], t0[:, :, :], tile_first[:, :, :], ALU.add))
            bits(t1, t0, 3, None, AND)
            step(nc.vector.tensor_copy(di[:, :, :], t1[:, :, :]))
            bits(t2, t0, 2, None, SHR)
            step(nc.vector.tensor_copy(dq[:, :, :], t2[:, :, :]))
            step(nc.vector.scalar_tensor_tensor(dcode[:, :, :], t1[:, :, :], 64.0, t2[:, :, :], ALU.mult, ALU.add))
            bits(t0, sidx, 2, P - 1, SHR, AND)
            step(nc.vector.tensor_copy(srow[:, :, :], t0[:, :, :]))
            bits(t1, sidx, 9, 2, SHR, SHL)
            bits(t2, sidx, 3, None, AND)
            step(nc.vector.tensor_tensor(scol[:, :, :], t1[:, :, :], t2[:, :, :], ALU.add))
            step(nc.vector.scalar_tensor_tensor(nidx[:, :, :], srow[:, :, :], float(G * B), scol[:, :, :], ALU.mult, ALU.add))
            dve.sem_inc(slots_set, 1)
            def hots(t, k):
                wait(dve, f_hist, t - 3)
                of = bass.ds(t, 1)
                nc.vector.tensor_scalar(hot[k % 2][:, k // 2, :], iota_b[:, 0:P], srow[:, :, :].rearrange("p h g -> p (h g)")[:, of], None, ALU.is_equal)
                nc.vector.tensor_scalar(hotc[k % 2][:, k // 2, :], iota_c[:, :], scol[:, :, :].rearrange("p h g -> p (h g)")[:, of], None, ALU.is_equal).then_inc(f_hot, 1)

            def places(h):
                step(nc.vector.tensor_tensor(hp[:, :, :], iota_b[:, 0:64].rearrange("p (o q) -> p o q", o=1).to_broadcast([P, G, 64]),
                                             dq[:, h, :].rearrange("p (g o) -> p g o", o=1).to_broadcast([P, G, 64]), ALU.is_equal))
                nc.vector.tensor_tensor(hi[:, :, :], iota_b[:, 0:B].rearrange("p (o q) -> p o q", o=1).to_broadcast([P, G, B]),
                                        di[:, h, :].rearrange("p (g o) -> p g o", o=1).to_broadcast([P, G, B]), ALU.is_equal).then_inc(f_hp, 1)
            dve.wait_ge(f_clean, 9)
            places(0)
            for k in range(4):
                hots(k, k)
            dve.wait_ge(f_in, 1)
            places(1)
            with dve.Fori(0, (T - 4) // 8) as i:
                for k in range(8):
                    hots(8 * i + (4 + k), k % 4)
            dve.wait_ge(f_hist, T)
            step(nc.vector.tensor_scalar(deg_out[:, :], pA[1][:, 0:G * B], 1.0, None, ALU.add))
            nc.vector.reciprocal(nsrc[:, :], deg_out[:, :]).then_inc(f_recip, 1)
            dve.wait_ge(f_in, 2)
            step(nc.vector.tensor_scalar(deg_in[:, :], pD[0][:, 0:G * B], 1.0, None, ALU.add))
            nc.vector.reciprocal(ndst[:, :], deg_in[:, :]).then_inc(f_recip, 1)
            dve.wait_ge(f_degt, 1)
            for c in range(4):
                m = min(P, G * B - c * P)
                nc.vector.tensor_copy(degT16[0:m, c, :], pB[0][0:m, c * P:(c + 1) * P]).then_inc(f_deg16, 1)
            dve.wait_ge(f_fuse_pe, 1)
            nc.vector.tensor_copy(we2T[:, :], pB[1][:, 0:D])
            nc.vector.tensor_tensor(wes[:, :], we1a[:, :], we1b[:, :], ALU.add).then_inc(f_fuse, 1)
            dve.wait_ge(f_fuse_pe, 2)
            nc.vector.tensor_copy(wf[:, :], pB[1][:, 128:128 + D])
            step(nc.vector.tensor_copy(vrow[:, :], pB[1][0:1, 256:256 + D]))
            for v, row in enumerate((vrow, be1r)):
                step(nc.vector.tensor_copy(vparts[:, 0 + v, :], row[:, :]))
                step(nc.vector.tensor_tensor(vres[:, 0, :], row[:, :], vparts[:, 0 + v, :], ALU.subtract))
                step(nc.vector.tensor_copy(vparts[:, 2 + v, :], vres[:, 0, :]))
                step(nc.vector.tensor_tensor(vres[:, 1, :], vres[:, 0, :], vparts[:, 2 + v, :], ALU.subtract))
                step(nc.vector.tensor_copy(vparts[:, 4 + v, :], vres[:, 1, :]))
            dve.sem_inc(f_parts, 1)
            dve.wait_ge(f_norm, 2)

            def per_group(v, g):
                return v[:, bass.ds(g.g * B, B)].rearrange("p (i o) -> p i o", o=1).to_broadcast([P, B, D])

            def bias(v):
                return v[:, :].rearrange("p (o d) -> p o d", o=1).to_broadcast([P, B, D])

            for s in range(3):
                ph = phases[s]
                if s:
                    tables_complete(dve, s - 1)
                per = (1, 3, 3)[s]
                base = n[0]

                def hot_rows(g, s=s, ph=ph):
                    after(dve, ph.summed if s == 0 else ph.rsum, g, 2)
                    if s == 0:
                        dve.wait_ge(ph.x_in[g.r], 16 * g.u + 16)
                        nc.vector.tensor_tensor(v3(mT[g.b][:, :]), fx[g.r][:, :, :], per_group(nsrc, g), ALU.mult)
                    for h in range(2):
                        c = dcode[:, h, bass.ds(g.g, 1)]
                        last = nc.vector.tensor_scalar((hot16 if s == 2 else fhot)[g.b][:, h, :], iota_b[:, :], c, None, ALU.is_equal)
                    last.then_inc(ph.hot_set, 1)

                def linked(g, k, per=per, base=base):
                    dve.wait_ge(chain, g.g * per + (base + k))

                def link(g, k, ins, linked=linked):
                    ins.then_inc(chain, 1)
                    linked(g, k)

                def post(g, s=s, ph=ph, link=link):
                    if s == 0:
                        after(dve, ph.scaled, g)
                        link(g, 1, nc.vector.tensor_tensor(z[g.b][:, :, :], z[g.b][:, :, :], bias(b1b), ALU.add))
                        wait(dve, ph.stored[g.r], 16 * g.u)
                        nc.vector.scalar_tensor_tensor(fo[g.r][:, :, :], z[g.b][:, :, :], 0.0, per_group(nsrc, g), ALU.max, ALU.mult).then_inc(ph.result, 1)
                        return
                    after(dve, ph.outp, g)
                    link(g, 1, nc.vector.tensor_tensor(z[g.b][:, :, :], v3(pD[g.b][:, :]), bias(bn2b), ALU.add))
                    after(dve, ph.result, g, 4)
                    link(g, 2, nc.vector.scalar_tensor_tensor(fy[g.r][:, :, :], fx[g.r][:, :, :], 2.0, z[g.b][:, :, :], ALU.mult, ALU.add))
                    for i in range(B):
                        last = nc.vector.bn_stats(fst[g.r][:, i, :], fy[g.r][:, i, :])
                    link(g, 3, last)
                    dve.sem_inc(held_dve, 1)
                    for i in range(B):
                        last = nc.vector.bn_aggr(fmv[g.r][:, i, :], fst[g.r][:, i, :])
                    last.then_inc(ph.posted, 1)

                def invert_root(g, ph=ph):
                    after(dve, ph.rooted, g)
                    nc.vector.reciprocal(frs[g.r][:, :], fsd[g.r][:, :]).then_inc(ph.recip, 1)

                def invert_mean(g, ph=ph):
                    after(dve, ph.recip, g)
                    nc.vector.scalar_tensor_tensor(fnm[g.r][:, :], fmv[g.r][:, :, 0], -1.0, frs[g.r][:, :], ALU.mult, ALU.mult).then_inc(ph.inverted, 1)

                def second_body(at, ph=ph, linked=linked):
                    ahead, g, behind = at(3), at(0), at(-1)

                    def one_hot(h):
                        return nc.vector.tensor_scalar(fhot[ahead.b][:, h, :], iota_b[:, :], dcode[:, h, bass.ds(ahead.g, 1)], None, ALU.is_equal)
                    if ahead:
                        after(dve, ph.summed, ahead, 2)
                        one_hot(0)
                    if g:
                        after(dve, ph.scaled, g)
                        nc.vector.tensor_tensor(z[g.b][:, :, :], z[g.b][:, :, :], bias(b2b), ALU.add).then_inc(chain, 1)
                    if ahead:
                        one_hot(1).then_inc(ph.hot_set, 1)
                    if g:
                        dve.wait_ge(ph.x2_in[g.r], 16 * g.u + 16)
                        after(dve, ph.result, g, 4)
                        linked(g, 1)
                        nc.vector.scalar_tensor_tensor(fy[g.r][:, :, :], z[g.b][:, :, :], 0.0, fx2[g.r][:, :, :], ALU.max, ALU.add).then_inc(chain, 1)
                    if behind:
                        invert_root(behind)
                    if g:
                        linked(g, 2)
                        for i in range(B):
                            last = nc.vector.bn_stats(fst[g.r][:, i, :], fy[g.r][:, i, :])
                        last.then_inc(chain, 1)
                    if behind:
                        invert_mean(behind)
                    if g:
                        linked(g, 3)
                        dve.sem_inc(held_dve, 1)
                        for i in range(B):
                            last = nc.vector.bn_aggr(fmv[g.r][:, i, :], fst[g.r][:, i, :])
                        last.then_inc(ph.posted, 1)

                def split(g, ph=ph):
                    first, second, third = mparts[g.b]
                    after(dve, ph.msgs, g)
                    nc.vector.tensor_tensor(fm[g.b][:, :, :], fm[g.b][:, :, :], first, ALU.subtract).then_inc(ph.rest, 1)
                    after(dve, ph.rsum, g, 2)
                    dve.wait_ge(ph.rest, 2 * g.g + 1)
                    nc.vector.tensor_copy(second, fm[g.b][:, :, :]).then_inc(ph.rest, 1)
                    dve.wait_ge(ph.rest, 2 * g.g + 2)
                    nc.vector.tensor_tensor(third, fm[g.b][:, :, :], second, ALU.subtract).then_inc(ph.parted, 1)

                def body(at, s=s, ph=ph):
                    if s == 2 and at(0):
                        g = at(0)
                        after(dve, ph.rsum, g)
                        after(dve, ph.scaled, g)
                        after(dve, ph.hid, g, 2)
                        nc.vector.tensor_tensor(aT[g.b][:, :], pC[0][:, :], fs[g.b][:, :], ALU.add).then_inc(ph.radd, 1)
                    if at(3 if s == 0 else 2):
                        hot_rows(at(3 if s == 0 else 2))
                    if at(0 if s == 0 else -1):
                        post(at(0 if s == 0 else -1))
                    if s == 2 and at(1):
                        split(at(1))
                    if s == 2 and at(-2):
                        invert_root(at(-2))
                        invert_mean(at(-2))
                pipeline(dve, second_body if s == 1 else body, 3 if s < 2 else 2, (0, 1, 2)[s])
                n[0] += per * G

        def fast_scalar(act):
            act.wait_ge(f_recip, 1)
            nc.scalar.activation(nsrc[:, :], nsrc[:, :], ACT.Sqrt).then_inc(f_norm, 1)
            act.wait_ge(f_recip, 2)
            nc.scalar.activation(ndst[:, :], ndst[:, :], ACT.Sqrt).then_inc(f_norm, 1)
            act.wait_ge(f_norm, 2)
            act.wait_ge(loaded, 16 * LOADS)
            act.wait_ge(early_in, 16 * 2 * EARLY)
            for s in range(3):
                ph = phases[s]
                if s:
                    tables_complete(act, s - 1)

                def normalise(g, ph=ph):
                    after(act, ph.inverted, g)
                    wait(act, ph.stored[g.r], 16 * g.u)
                    for i in range(B):
                        last = nc.scalar.activation(fo[g.r][:, i, :], fy[g.r][:, i, :], ACT.Identity,
                                                    scale=frs[g.r][:, i:i + 1], bias=fnm[g.r][:, i:i + 1])
                    last.then_inc(ph.result, 1)

                def root(g, ph=ph):
                    after(act, ph.posted, g)
                    nc.scalar.activation(fsd[g.r][:, :], fmv[g.r][:, :, 1], ACT.Sqrt, bias=eps[:, 0:1]).then_inc(ph.rooted, 1)

                def evacuate(g, s=s, ph=ph):
                    after(act, ph.summed, g)
                    if s < 2:
                        after(act, ph.mixed, g, 2)
                        nc.scalar.copy(aT[g.b][:, :], pA[g.b][:, :]).then_inc(ph.evacuated, 1)
                    else:
                        after(act, ph.hid, g, 2)
                        nc.scalar.copy(xT[g.b][:, :], pA[0][:, :])
                        nc.scalar.copy(fe[g.b][:, :], pA[1][:, :]).then_inc(ph.evacuated, 1)

                def messages(g, ph=ph):
                    landed(act, ph.gathered, g, 2)
                    after(act, ph.summed, g, 2)
                    for h in range(2):
                        last = nc.scalar.activation(fm[g.b][:, h, :], early[:, bass.ds(g.g, 1), h, :].rearrange("p o d -> p (o d)"),
                                                    ACT.Identity, scale=fn[g.r][:, h:h + 1])
                    last.then_inc(ph.scaled_msg, 1)

                def body(at, s=s, ph=ph, root=root, normalise=normalise, evacuate=evacuate, messages=messages):
                    if s < 2:
                        g = at(0)
                        if g:
                            after(act, ph.mixed, g)
                            after(act, ph.result if s == 0 else ph.posted, g, 2)
                            for i in range(B):
                                last = nc.scalar.activation(z[g.b][:, i, :], pB[g.b][:, i * D:(i + 1) * D], ACT.Identity,
                                                            scale=ndst[:, bass.ds(g.g * B + i, 1)])
                            last.then_inc(ph.scaled, 1)
                        if at(2):
                            evacuate(at(2))
                        if s == 0 and at(3):
                            messages(at(3))
                        if s == 1 and at(-2):
                            normalise(at(-2))
                        if s == 1 and at(-1):
                            root(at(-1))
                        return
                    if at(1):
                        evacuate(at(1))
                    if at(-2):
                        root(at(-2))
                    if at(-3):
                        normalise(at(-3))
                    g = at(1)
                    if g:
                        after(act, ph.mixed, g)
                        after(act, ph.rsum, g, 2)
                        nc.scalar.activation(fm[g.b][:, :, :], pB[1][:, 0:2 * D].rearrange("p (h d) -> p h d", h=2), ACT.Relu)
                        nc.scalar.activation(mparts[g.b][0], pB[1][:, 0:2 * D].rearrange("p (h d) -> p h d", h=2), ACT.Relu).then_inc(ph.msgs, 1)
                        after(act, ph.radd, g, 2)
                        nc.scalar.activation(fs[g.b][:, :], pB[0][:, :], ACT.Relu, bias=be1c[:, 0:1]).then_inc(ph.scaled, 1)
                    g = at(0)
                    if g:
                        after(act, ph.hid, g)
                        after(act, ph.outp, g, 2)
                        nc.scalar.activation(mT[g.b][:, :], pC[1][:, :], ACT.Relu, bias=bn1c[:, 0:1]).then_inc(ph.hidact, 1)
                pipeline(act, body, (3, 2, 1)[s], (0, 2, 3)[s], 1,
                         [((EARLY - 3) // 4, lambda: act.wait_ge(late_in[0], 16 * 2 * (LATER - EARLY))),
                          ((LATER - 3) // 4, lambda: act.wait_ge(late_in[1], 16 * 2 * (G - LATER)))] if s == 0 else ())

        def fast_tensor(pe):
            pe.wait_ge(keys_set, 1)
            for h in range(2):
                last = nc.tensor.transpose(pA[0][:, h * G:(h + 1) * G], keys[0:G, h, :], ident[0:G, 0:G])
            last.then_inc(keys_turned, 1)
            def hist(t, k, start=False, stop=False):
                pe.wait_ge(f_hot, t + 1)
                nc.tensor.matmul(pA[1][:, 0:G * B], hot[k % 2][:, k // 2, :], hotc[k % 2][:, k // 2, :], start=start, stop=stop).then_inc(f_hist, 1)

            def degrees_in(h):
                pe.wait_ge(f_hp, h + 1)
                for g in range(G):
                    last = nc.tensor.matmul(pD[0][64 * h:64 * h + 64, B * g:B * g + B], hp[:, g, :], hi[:, g, :], start=True, stop=True)
                last.then_inc(f_in, 1)
            degrees_in(0)
            for k in range(4):
                hist(k, k, start=k == 0)
            degrees_in(1)
            with pe.Fori(0, (T - 4) // 8 - 1) as i:
                for k in range(8):
                    hist(8 * i + (4 + k), k % 4)
            for k in range(8):
                hist(T - 8 + k, k % 4, stop=k == 7)
            pe.wait_ge(f_recip, 2)
            for c in range(4):
                m = min(P, G * B - c * P)
                last = nc.tensor.transpose(pB[0][0:m, c * P:(c + 1) * P], deg_in[:, c * P:c * P + m], ident[:, :])
            last.then_inc(f_degt, 1)
            nc.tensor.transpose(pB[1][:, 0:D], we2[:, :], ident[:, :]).then_inc(f_fuse_pe, 1)
            pe.wait_ge(f_fuse, 1)
            nc.tensor.matmul(pB[1][:, 128:128 + D], we2T[:, :], wn1b[:, :], start=True, stop=True)
            nc.tensor.matmul(pB[1][0:1, 256:256 + D], be2c[:, :], wn1b[:, :], start=True, stop=True).then_inc(f_fuse_pe, 1)

            def halves(t, h):
                return t[:, :].rearrange("p (i h q) -> p h i q", i=B, h=2)[:, h]

            for s in range(3):
                ph = phases[s]
                if s:
                    tables_complete(pe, s - 1)
                if s == 0:
                    pe.wait_ge(f_parts, 1)
                    pe.wait_ge(f_deg16, 4)
                if s == 2:
                    pe.wait_ge(f_parts_in, 32)

                def sums(dest, rows, ones_of, first, final):
                    for h in range(2):
                        last = nc.tensor.matmul(halves(dest, h), rows[:, h, :], ones_of[:, h, :].rearrange("p (i q) -> p i q", i=B),
                                                start=first and h == 0, stop=final and h == 1, skip_group_check=True)
                    return last

                def stage_a(g, s=s, ph=ph, sums=sums):
                    if s < 2:
                        after(pe, ph.hot_set, g)
                        pe.wait_ge(ph.x_in[g.r], 16 * g.u + 16)
                        if s == 0:
                            after(pe, ph.scaled_msg, g)
                        else:
                            landed(pe, ph.gathered, g, 2)
                        after(pe, ph.evacuated, g, 2)
                        for i in range(B):
                            nc.tensor.matmul(pA[g.b][:, i * P:(i + 1) * P], (v3(mT[g.b][:, :]) if s == 0 else fx[g.r])[:, i, :], ident[:, :],
                                             start=i == 0, stop=False, is_transpose=True, skip_group_check=True)
                        sums(pA[g.b], fr[g.r] if s else fm[g.b], fhot[g.b], False, True).then_inc(ph.summed, 1)
                        return
                    pe.wait_ge(ph.x_in[g.r], 16 * g.u + 16)
                    landed(pe, ph.gathered, g, 4)
                    after(pe, ph.evacuated, g, 1)
                    for i in range(B):
                        nc.tensor.transpose(pA[0][:, i * P:(i + 1) * P], fx[g.r][:, i, :], ident[:, :])
                        last = nc.tensor.transpose(pA[1][:, i * P:(i + 1) * P], fr[g.r][:, i, :], ident[:, :])
                    last.then_inc(ph.summed, 1)

                def stage_b(g, s=s, ph=ph):
                    after(pe, ph.evacuated, g)
                    if s < 2:
                        after(pe, ph.scaled, g, 2)
                        for i in range(B):
                            last = nc.tensor.matmul(pB[g.b][:, i * P:(i + 1) * P], aT[g.b][:, i * P:(i + 1) * P],
                                                    (w1 if s == 0 else w2)[:, :], start=True, stop=True)
                        last.then_inc(ph.mixed, 1)
                        return
                    after(pe, ph.scaled, g, 1)
                    nc.tensor.matmul(pB[0][:, :], wes[:, :], xT[g.b][:, :], start=True, stop=True)
                    for h in range(2):
                        m = pB[1][:, h * D:(h + 1) * D]
                        nc.tensor.matmul(m, onesb[0:3, :], vp3[:, 1, :], start=True, stop=False)
                        nc.tensor.matmul(m, fe[g.b][:, h * P:(h + 1) * P], we1a[:, :], start=False, stop=False)
                        last = nc.tensor.matmul(m, fe[g.b][:, (2 + h) * P:(3 + h) * P], we1b[:, :], start=False, stop=True)
                    last.then_inc(ph.mixed, 1)

                def body(at, s=s, ph=ph, stage_a=stage_a, stage_b=stage_b, sums=sums):
                    if s < 2:
                        if at(0):
                            stage_b(at(0))
                        if at(2):
                            stage_a(at(2))
                        return
                    if at(1):
                        stage_a(at(1))
                    g = at(0)
                    if g:
                        after(pe, ph.hot_set, g)
                        after(pe, ph.parted, g)
                        after(pe, ph.radd, g, 1)
                        for k, part in enumerate(mparts[g.b]):
                            last = sums(pC[0], part, hot16[g.b], k == 0, k == 2)
                        last.then_inc(ph.rsum, 1)
                    g = at(-1)
                    if g:
                        after(pe, ph.hidact, g)
                        after(pe, ph.posted, g, 2)
                        for i in range(B):
                            last = nc.tensor.matmul(pD[g.b][:, i * P:(i + 1) * P], mT[g.b][:, i * P:(i + 1) * P], wn2[:, :], start=True, stop=True)
                        last.then_inc(ph.outp, 1)
                    if at(1):
                        stage_b(at(1))
                    g = at(0)
                    if g:
                        nc.tensor.matmul(pC[1][:, :], wn1a[:, :], xT[g.b][:, :], start=True, stop=False)
                        after(pe, ph.radd, g)
                        nc.tensor.matmul(pC[1][:, :], wf[:, :], aT[g.b][:, :], start=False, stop=False)
                        pe.wait_ge(ph.d_in[g.r], 16 * g.u + 16)
                        nc.tensor.matmul(pC[1][:, :], vp3[:, 0, :], fd[g.r][:, :], start=False, stop=True).then_inc(ph.hid, 1)
                pipeline(pe, body, 2 if s < 2 else 1, 1 if s == 2 else 0)
        block = ctx.enter_context(nc.Block())

        @block.sync
        def _(sp):
            sp.dma_start(src_i[:, :], src.rearrange("(p t) -> p t", p=EP)).then_inc(loaded, 16)
            sp.dma_start(dst_i[:, :], dst.rearrange("(p t) -> p t", p=EP)).then_inc(loaded, 16)
            for w, a in ((w1, W1), (w2, W2), (we1a, We1[0:P, :]), (we1b, We1[P:2 * P, :]), (we2, We2),
                         (wn1a, Wn1[0:P, :]), (wn1b, Wn1[P:2 * P, :]), (wn2, Wn2)):
                sp.dma_start(w[:, :], a).then_inc(loaded, 16)
            with nc.allow_non_contiguous_dma(reason="bias columns"):
                sp.dma_start(be2c[:, :], be2.rearrange("(p o) -> p o", o=1)).then_inc(loaded, 16)
                sp.dma_start(bn1c[:, :], bn1.rearrange("(p o) -> p o", o=1)).then_inc(loaded, 16)
            for w, a in ((b1b, b1), (b2b, b2), (be1b, be1), (bn2b, bn2)):
                sp.dma_start(w[:, :], a.rearrange("(o d) -> o d", o=1).to_broadcast([P, D])).then_inc(loaded, 16)
            with nc.allow_non_contiguous_dma(reason="bias columns"):
                sp.dma_start(be1c[:, :], be1.rearrange("(p o) -> p o", o=1)).then_inc(loaded, 16)
            sp.dma_start(be1r[:, :], be1.rearrange("(o d) -> o d", o=1)).then_inc(loaded, 16)
            sp.wait_ge(verdict_set, 1)
            regular = sp.value_load(regular_i[0:1, 0:1], min_val=0, max_val=1)
            with sp.If(regular == 1):
                fast_sync(sp)
            with sp.Else():
                slow_sync(sp)

        @block.gpsimd
        def _(pool):
            nc.gpsimd.memset(ones[:, :], 1.0).then_inc(consts, 1)
            nc.gpsimd.memset(eps[:, :], EPS).then_inc(consts, 1)
            nc.gpsimd.iota(iota_c[:, :], [[1, G * B]], base=0, channel_multiplier=0, allow_small_or_imprecise_dtypes=True).then_inc(consts, 1)
            nc.gpsimd.iota(iota_p[:, :], [[0, 1]], base=0, channel_multiplier=1, allow_small_or_imprecise_dtypes=True).then_inc(consts, 1)
            nc.gpsimd.iota(trash[:, :], [[0, 1]], base=TRASH, channel_multiplier=1, allow_small_or_imprecise_dtypes=True).then_inc(consts, 1)
            pool.wait_ge(consts, 5)
            nc.gpsimd.affine_select(out=ident[:, :], in_=ones[:, :], compare_op=ALU.is_equal, fill=0.0,
                                    base=0, pattern=[[-1, P]], channel_multiplier=1).then_inc(consts, 1)
            nc.gpsimd.affine_select(out=lower[:, :], in_=ones[:, :], compare_op=ALU.is_gt, fill=0.0,
                                    base=0, pattern=[[-1, P]], channel_multiplier=1).then_inc(consts, 1)
            nc.gpsimd.affine_select(out=upper[:, :], in_=ones[:, :], compare_op=ALU.is_gt, fill=0.0,
                                    base=0, pattern=[[1, P]], channel_multiplier=-1).then_inc(consts, 1)
            nc.gpsimd.memset(onesb[:, :], 1.0).then_inc(consts, 1)
            nc.gpsimd.memset(check[:, :], 0.0).then_inc(consts, 1)
            nc.gpsimd.iota(tile_first[:, :, :], [[HN, 2], [GN, G]], base=0, channel_multiplier=0, allow_small_or_imprecise_dtypes=True).then_inc(consts, 1)
            nc.gpsimd.iota(my_first[:, :], [[HN, 2]], base=0, channel_multiplier=GN, allow_small_or_imprecise_dtypes=True).then_inc(consts, 1)
            nc.gpsimd.iota(iota_b[:, :], [[1, HN]], base=0, channel_multiplier=0, allow_small_or_imprecise_dtypes=True).then_inc(consts, 1)
            pool.wait_ge(first_set, 1)
            pool.wait_ge(win_built, 64)
            for k in range(2):
                for h in range(2):
                    nc.gpsimd.indirect_dma_start(out=win_i[k][0:G, h, :], out_offset=None, in_=win_tab[k][:, :],
                                                 in_offset=bass.IndirectOffsetOnAxis(ap=first_i[0:G, h:h + 1], axis=0)).then_inc(win_in, 16)
            pool.wait_ge(verdict_set, 1)
            regular = pool.value_load(regular_i[0:1, 0:1], min_val=0, max_val=1)
            with pool.If(regular == 1):
                fast_pool(pool)
            with pool.Else():
                slow_pool(pool)

        @block.vector
        def _(dve):
            n = [0]

            def step(ins):
                n[0] += 1
                ins.then_inc(chain, 1)
                dve.wait_ge(chain, n[0])

            step(nc.vector.memset(early_flat[96:P, 0:12 * CW], 0.0))
            dve.wait_ge(loaded, 16 * LOADS)
            dve.wait_ge(consts, 7)
            dve.wait_ge(consts, 13)
            for k, v in enumerate((src_i, dst_i)):
                nc.vector.tensor_copy(edge_f[k][:, :], v[:, :])
            step(nc.vector.memset(rt[:, :], 0.0))
            for j in range(5):
                last = nc.vector.tensor_scalar(below[:, j, :, :], tile_first[0:EP, :, :], edge_f[1][:, j * CS:j * CS + 1], None, ALU.is_gt)
            last.then_inc(below_set, 1)
            step(nc.vector.tensor_tensor(loop[:, :], edge_f[0][:, :], edge_f[1][:, :], ALU.is_equal))
            step(nc.vector.tensor_tensor_scan(rank[:, :], loop[:, :], loop[:, :], 0.0, ALU.add, ALU.max))
            nc.vector.tensor_copy(check[0:EP, 3:4], rank[:, ET - 1:ET]).then_inc(ranked, 1)
            dve.wait_ge(counted, 1)
            step(nc.vector.tensor_scalar(first_win[0:G, :], pD[1][0:G, 0:2], -1.0, 0.0, ALU.add, ALU.max))
            nc.vector.tensor_scalar(first_i[0:G, :], first_win[0:G, :], float(CL), None, ALU.min).then_inc(first_set, 1)
            dve.wait_ge(rank_off, 1)
            step(nc.vector.tensor_scalar(off1[0:EP, :], pD[0][0:EP, 0:1], -1.0, None, ALU.add))
            step(nc.vector.scalar_tensor_tensor(rank[:, :], rank[:, :], off1[0:EP, 0:1], edge_f[1][:, :], ALU.add, ALU.not_equal))
            step(nc.vector.tensor_tensor_reduce(out=edge_f[0][:, :], in0=rank[:, :], in1=loop[:, :], scale=1.0, scalar=0.0,
                                                op0=ALU.mult, op1=ALU.add, accum_out=check[0:EP, 0:1]))
            dve.wait_ge(win_in, 64)
            for k in range(2):
                last = nc.vector.tensor_copy(win_f[k][0:G, :, :], win_i[k][0:G, :, :])
            step(last)
            nc.vector.tensor_tensor(wa[0:G, :, :], win_f[0][0:G, :, :], win_f[1][0:G, :, :], ALU.not_equal)
            for h in range(2):
                last = nc.vector.tensor_scalar(wb[0:G, h, :], win_f[1][0:G, h, :], my_first[0:G, h:h + 1], None, ALU.subtract)
            step(last)
            step(nc.vector.scalar_tensor_tensor(wa[0:G, :, :], wb[0:G, :, :], 0.0, wa[0:G, :, :], ALU.is_ge, ALU.mult))
            step(nc.vector.scalar_tensor_tensor(wa[0:G, :, :], wb[0:G, :, :], float(HN), wa[0:G, :, :], ALU.is_lt, ALU.mult))
            step(nc.vector.tensor_reduce(check[0:G, 4:6], wa[0:G, :, :], mybir.AxisListType.X, ALU.add))
            step(nc.vector.scalar_tensor_tensor(wb[0:G, :, :], wb[0:G, :, :], float(KEY), win_f[0][0:G, :, :], ALU.mult, ALU.add))
            step(nc.vector.scalar_tensor_tensor(wb[0:G, :, :], wb[0:G, :, :], 1.0, wa[0:G, :, :], ALU.add, ALU.mult))
            step(nc.vector.tensor_scalar(wa[0:G, :, :], wb[0:G, :, :], -1.0, None, ALU.add))
            step(nc.vector.tensor_tensor(check[0:G, 2:3], check[0:G, 4:5], check[0:G, 5:6], ALU.add))
            step(nc.vector.tensor_scalar(off1[0:G, :], check[0:G, 4:5], float(SLOTS), None, ALU.is_gt))
            step(nc.vector.scalar_tensor_tensor(check[0:G, 1:2], check[0:G, 5:6], float(SLOTS), off1[0:G, :], ALU.is_gt, ALU.add))
            dve.sem_inc(checked, 1)
            dve.wait_ge(check_sum, 1)
            for k, want in enumerate((0, 0, E - N, N)):
                last = nc.vector.tensor_scalar(verdict[:, k:k + 1], pD[0][0:1, 8 + k:9 + k], float(want), None, ALU.is_equal)
            step(last)
            nc.vector.tensor_reduce(regular_i[:, 0:1], verdict[:, 0:4], mybir.AxisListType.X, ALU.min).then_inc(verdict_set, 1)
            dve.wait_ge(verdict_set, 1)
            regular = dve.value_load(regular_i[0:1, 0:1], min_val=0, max_val=1)
            with dve.If(regular == 1):
                fast_vector(dve, list(n))
            with dve.Else():
                slow_vector(dve, n, step)

        @block.scalar
        def _(act):
            for k, v in enumerate((src, dst)):
                act.dma_start(win_tab[k][0:CL, :], bass.AP(v.tensor, v.offset, [[CS, CL], [1, CW]])).then_inc(win_built, 16)
                act.dma_start(win_tab[k][CL:CL + 1, :], v[E - CW:E].rearrange("(o n) -> o n", o=1)).then_inc(win_built, 16)
            act.wait_ge(verdict_set, 1)
            regular = act.value_load(regular_i[0:1, 0:1], min_val=0, max_val=1)
            with act.If(regular == 1):
                fast_scalar(act)
            with act.Else():
                slow_scalar(act)

        @block.tensor
        def _(pe):
            pe.wait_ge(consts, 13)
            pe.wait_ge(below_set, 1)
            for h in range(2):
                for j in range(5):
                    last = nc.tensor.matmul(pD[1][0:G, h:h + 1], below[:, j, h, :], onesb[0:EP, 0:1], start=j == 0, stop=j == 4)
            last.then_inc(counted, 1)
            pe.wait_ge(ranked, 1)
            nc.tensor.matmul(pD[0][:, 0:1], upper[0:EP, :], check[0:EP, 3:4], start=True, stop=True).then_inc(rank_off, 1)
            pe.wait_ge(checked, 1)
            nc.tensor.matmul(pD[0][:, 8:12], ones[:, :], check[:, 0:4], start=True, stop=True).then_inc(check_sum, 1)
            pe.wait_ge(verdict_set, 1)
            regular = pe.value_load(regular_i[0:1, 0:1], min_val=0, max_val=1)
            with pe.If(regular == 1):
                fast_tensor(pe)
            with pe.Else():
                slow_tensor(pe)


_INS = ['x', 'src', 'dst', 'L0_gnn_W1', 'L0_gnn_b1', 'L0_gnn_W2', 'L0_gnn_b2', 'L1_gnn_We1', 'L1_gnn_be1', 'L1_gnn_We2',
        'L1_gnn_be2', 'L1_gnn_Wn1', 'L1_gnn_bn1', 'L1_gnn_Wn2', 'L1_gnn_bn2']


def kernel(**inputs):
    import numpy as _np
    import concourse.bacc as _bacc
    from concourse import mybir as _mybir
    from concourse.bass_utils import run_bass_kernel_spmd as _run

    nc = _bacc.Bacc("TRN2", target_bir_lowering=False, num_devices=1)
    arrays, args = {}, []
    for name in _INS:
        a = _np.ascontiguousarray(inputs[name])
        arrays[f"in_{name}_dram"] = a
        args.append(nc.dram_tensor(f"in_{name}_dram", a.shape, _mybir.dt.from_np(a.dtype), kind="ExternalInput").ap())
    args.append(nc.dram_tensor("out_0_dram", args[0].shape, F32, kind="ExternalOutput").ap())
    gnn(nc, *args)
    r = _run(nc, [arrays], core_ids=[0])
    return r.results[0]["out_0_dram"]
```
